# Optimizing a Trainium2 kernel written in Bass

```python
import numpy as np
import jax
import jax.numpy as jnp

def _softmax(x, axis=-1):
    return jax.nn.softmax(x, axis=axis)

def _gelu(x):
    return jax.nn.gelu(x, approximate=True)

def _silu(x):
    return jax.nn.silu(x)

def _sigmoid(x):
    return jax.nn.sigmoid(x)

def _layernorm(x, axis=-1, eps=1e-05):
    m = jnp.mean(x, axis=axis, keepdims=True)
    v = jnp.var(x, axis=axis, keepdims=True)
    return (x - m) / jnp.sqrt(v + eps)

def _scatter_add(tgt, idx, src, axis=0):
    return tgt.at[idx].add(src)

def _segment_sum(src, seg, n):
    return jax.ops.segment_sum(src, seg, n)
kernel_name = 'mk_lm_tower_d1_tok_ids256_r4_c5d1f5'

def setup_inputs(seed: int=0):
    np.random.seed(seed)
    _w = jnp.asarray

    def _rec_inputs():
        import jax
        import jax.numpy as jnp
        _rk = jax.random.key(seed)
        x = jax.random.randint(jax.random.fold_in(_rk, 1), (2, 2048), 0, 50226, jnp.int32)
        return x
    x = _rec_inputs()

    def _L0_tok_setup():
        import jax, jax.numpy as jnp
        import numpy as np
        VOCAB = 50257
        EMBED = 64
        NFREQ = 64
        NRULES = 100
        B, S = (4, 256)
        key = jax.random.key(seed)
        ks = jax.random.split(key, 7)
        return {'token_ids': jax.random.randint(ks[0], (B, S), 0, VOCAB), 'a_n': jax.random.normal(ks[1], (VOCAB, NFREQ), dtype=jnp.float32), 'b_n': jax.random.normal(ks[2], (VOCAB, NFREQ), dtype=jnp.float32), 'rule_transform': jax.random.normal(ks[3], (NRULES, EMBED, EMBED), dtype=jnp.float32), 'token_rules': jax.random.randint(ks[4], (VOCAB,), 0, NRULES), 'proj_w': jax.random.normal(ks[5], (EMBED, NFREQ), dtype=jnp.float32) * (1.0 / np.sqrt(NFREQ)), 'proj_b': jax.random.normal(ks[6], (EMBED,), dtype=jnp.float32) * 0.01}
    _L0_tok_all = _L0_tok_setup()
    _L0_tok_in = {k: v for k, v in _L0_tok_all.items() if k in ('a_n', 'b_n', 'rule_transform', 'token_rules', 'proj_w', 'proj_b')}
    del _L0_tok_all

    def _L0_attn_setup():
        import jax, jax.numpy as jnp
        import numpy as np
        N_HEADS, EMB, KQ = (8, 64, 64)
        BATCH, SEQ = (4, 512)
        key = jax.random.key(seed)
        ks = jax.random.split(key, 5)
        x = jax.random.normal(ks[0], (BATCH, SEQ, EMB), dtype=jnp.float32)
        key_matrices = 0.1 * jax.random.normal(ks[1], (N_HEADS, EMB, KQ), dtype=jnp.float32)
        query_matrices = 0.1 * jax.random.normal(ks[2], (N_HEADS, EMB, KQ), dtype=jnp.float32)
        value_in_matrices = 0.1 * jax.random.normal(ks[3], (N_HEADS, EMB, KQ), dtype=jnp.float32)
        value_out_matrices = 0.1 * jax.random.normal(ks[4], (N_HEADS, KQ, EMB), dtype=jnp.float32)
        return {'x': x, 'key_matrices': key_matrices, 'query_matrices': query_matrices, 'value_in_matrices': value_in_matrices, 'value_out_matrices': value_out_matrices}
    _L0_attn_all = _L0_attn_setup()
    _L0_attn_in = {k: v for k, v in _L0_attn_all.items() if k in ('key_matrices', 'query_matrices', 'value_in_matrices', 'value_out_matrices')}
    del _L0_attn_all

    def _L0_ffn_setup():
        import jax, jax.numpy as jnp
        import numpy as np
        DIM = 64
        HEADS = 8
        NUM_KEYS = 64
        NUM_KV = NUM_KEYS ** 2
        PK_TOPK = 16
        FINAL_TOPK = 16
        DIM_KEY = DIM // 2
        P = 2

        def _pk(x, Wq_pk, pk_keys):
            b, n, _ = x.shape
            q = (x @ Wq_pk).reshape(b, n, P, HEADS, DIM_KEY).transpose(2, 0, 1, 3, 4)
            sim = jnp.einsum('pbnhd,pkhd->pbnhk', q, pk_keys)
            scores, idx = jax.lax.top_k(sim, PK_TOPK)
            idx0 = idx[0]
            idx1 = idx[1] * NUM_KEYS
            index = (idx0[..., :, None] + idx1[..., None, :]).reshape(b, n, HEADS, PK_TOPK * PK_TOPK)
            score = (scores[0][..., :, None] + scores[1][..., None, :]).reshape(b, n, HEADS, PK_TOPK * PK_TOPK)
            final_scores, pk_idx = jax.lax.top_k(score, FINAL_TOPK)
            final_indices = jnp.take_along_axis(index, pk_idx, axis=-1)
            final_scores = jax.nn.softmax(final_scores, axis=-1)
            return (final_scores, final_indices)
        key = jax.random.key(seed)
        ks = jax.random.split(key, 7)
        b, n = (2, 256)
        std = 0.02
        x = jax.random.normal(ks[0], (b, n, DIM), dtype=jnp.float32)
        Wq_pk = jax.random.normal(ks[1], (DIM, P * HEADS * DIM_KEY), dtype=jnp.float32) * std
        pk_keys = jax.random.normal(ks[2], (P, NUM_KEYS, HEADS, DIM_KEY), dtype=jnp.float32) * std
        Wq = jax.random.normal(ks[3], (DIM, HEADS * DIM), dtype=jnp.float32) * std
        keys_table = jax.random.normal(ks[4], (NUM_KV * HEADS, DIM), dtype=jnp.float32) * std
        values_table = jax.random.normal(ks[5], (NUM_KV * HEADS, DIM), dtype=jnp.float32) * std
        Wo = jax.random.normal(ks[6], (DIM * HEADS, DIM), dtype=jnp.float32) * std
        return {'x': x, 'Wq_pk': Wq_pk, 'pk_keys': pk_keys, 'Wq': Wq, 'keys_table': keys_table, 'values_table': values_table, 'Wo': Wo}
    _L0_ffn_all = _L0_ffn_setup()
    _L0_ffn_in = {k: v for k, v in _L0_ffn_all.items() if k in ('Wq_pk', 'pk_keys', 'Wq', 'keys_table', 'values_table', 'Wo')}
    del _L0_ffn_all
    return {'x': x, 'L0_tok_a_n': _L0_tok_in['a_n'], 'L0_tok_b_n': _L0_tok_in['b_n'], 'L0_tok_rule_transform': _L0_tok_in['rule_transform'], 'L0_tok_token_rules': _L0_tok_in['token_rules'], 'L0_tok_proj_w': _L0_tok_in['proj_w'], 'L0_tok_proj_b': _L0_tok_in['proj_b'], 'L0_attn_key_matrices': _L0_attn_in['key_matrices'], 'L0_attn_query_matrices': _L0_attn_in['query_matrices'], 'L0_attn_value_in_matrices': _L0_attn_in['value_in_matrices'], 'L0_attn_value_out_matrices': _L0_attn_in['value_out_matrices'], 'L0_ffn_Wq_pk': _L0_ffn_in['Wq_pk'], 'L0_ffn_pk_keys': _L0_ffn_in['pk_keys'], 'L0_ffn_Wq': _L0_ffn_in['Wq'], 'L0_ffn_keys_table': _L0_ffn_in['keys_table'], 'L0_ffn_values_table': _L0_ffn_in['values_table'], 'L0_ffn_Wo': _L0_ffn_in['Wo']}

def reference(x, L0_tok_a_n, L0_tok_b_n, L0_tok_rule_transform, L0_tok_token_rules, L0_tok_proj_w, L0_tok_proj_b, L0_attn_key_matrices, L0_attn_query_matrices, L0_attn_value_in_matrices, L0_attn_value_out_matrices, L0_ffn_Wq_pk, L0_ffn_pk_keys, L0_ffn_Wq, L0_ffn_keys_table, L0_ffn_values_table, L0_ffn_Wo):
    import jax
    import jax.numpy as jnp

    def _L0_tok_ref(token_ids, a_n, b_n, rule_transform, token_rules, proj_w, proj_b):
        import jax, jax.numpy as jnp
        import numpy as np
        VOCAB = 50257
        EMBED = 64
        NFREQ = 64
        NRULES = 100
        B, S = (4, 256)
        vocab_size, nfreq = a_n.shape
        freqs = jnp.arange(1, nfreq + 1, dtype=jnp.float32)
        x = token_ids.astype(jnp.float32)[..., None] / vocab_size
        ang = 2.0 * jnp.pi * freqs * x
        fourier = a_n[token_ids] * jnp.cos(ang) + b_n[token_ids] * jnp.sin(ang)
        base = jnp.einsum('bsf,df->bsd', fourier, proj_w) + proj_b
        rule_idx = token_rules[token_ids]
        rules = rule_transform[rule_idx]
        return jnp.einsum('bsd,bsde->bse', base, rules)

    def _L0_attn_ref(x, key_matrices, query_matrices, value_in_matrices, value_out_matrices):
        import jax, jax.numpy as jnp
        import numpy as np
        N_HEADS, EMB, KQ = (8, 64, 64)
        BATCH, SEQ = (4, 512)
        seq_len = x.shape[1]
        queries = jnp.einsum('ned,bse->nbsd', query_matrices, x)
        keys = jnp.einsum('ned,bse->nbsd', key_matrices, x)
        kq = jnp.einsum('nbjd,nbkd->nbjk', keys, queries)
        mask = jnp.triu(jnp.ones((seq_len, seq_len), dtype=bool), k=1)
        kq = jnp.where(mask, -jnp.inf, kq)
        attention_pattern = jax.nn.softmax(kq, axis=3)
        v = jnp.einsum('bjp,npd->nbjd', x, value_in_matrices)
        ctx = jnp.einsum('nbsj,nbjd->nbsd', attention_pattern, v)
        return jnp.einsum('nbsd,nde->bse', ctx, value_out_matrices)

    def _L0_ffn_ref(x, Wq_pk, pk_keys, Wq, keys_table, values_table, Wo):
        import jax, jax.numpy as jnp
        import numpy as np
        DIM = 64
        HEADS = 8
        NUM_KEYS = 64
        NUM_KV = NUM_KEYS ** 2
        PK_TOPK = 16
        FINAL_TOPK = 16
        DIM_KEY = DIM // 2
        P = 2

        def _pk(x, Wq_pk, pk_keys):
            b, n, _ = x.shape
            q = (x @ Wq_pk).reshape(b, n, P, HEADS, DIM_KEY).transpose(2, 0, 1, 3, 4)
            sim = jnp.einsum('pbnhd,pkhd->pbnhk', q, pk_keys)
            scores, idx = jax.lax.top_k(sim, PK_TOPK)
            idx0 = idx[0]
            idx1 = idx[1] * NUM_KEYS
            index = (idx0[..., :, None] + idx1[..., None, :]).reshape(b, n, HEADS, PK_TOPK * PK_TOPK)
            score = (scores[0][..., :, None] + scores[1][..., None, :]).reshape(b, n, HEADS, PK_TOPK * PK_TOPK)
            final_scores, pk_idx = jax.lax.top_k(score, FINAL_TOPK)
            final_indices = jnp.take_along_axis(index, pk_idx, axis=-1)
            final_scores = jax.nn.softmax(final_scores, axis=-1)
            return (final_scores, final_indices)
        b, n, d = x.shape
        q = (x @ Wq).reshape(b, n, HEADS, DIM) * DIM ** (-0.5)
        kv_scores, indices = _pk(x, Wq_pk, pk_keys)
        offsets = jnp.arange(HEADS, dtype=indices.dtype) * NUM_KV
        ind = indices + offsets[None, None, :, None]
        k = jnp.einsum('bnhk,bnhkd->bnhd', kv_scores, keys_table[ind])
        v = jnp.einsum('bnhk,bnhkd->bnhd', kv_scores, values_table[ind])
        sim = jnp.einsum('bihd,bjhd->bhij', q, k)
        neg = -jnp.finfo(sim.dtype).max
        causal = jnp.tril(jnp.ones((n, n), dtype=bool))
        sim = jnp.where(causal, sim, neg)
        attn = jax.nn.softmax(sim, axis=-1)
        out = jnp.einsum('bhij,bjhd->bhid', attn, v)
        out = out.transpose(0, 2, 1, 3).reshape(b, n, HEADS * DIM)
        return out @ Wo
    h = _L0_tok_ref(x, L0_tok_a_n, L0_tok_b_n, L0_tok_rule_transform, L0_tok_token_rules, L0_tok_proj_w, L0_tok_proj_b)
    h = h + _L0_attn_ref(_layernorm(h, axis=-1), L0_attn_key_matrices, L0_attn_query_matrices, L0_attn_value_in_matrices, L0_attn_value_out_matrices)
    h = h + _L0_ffn_ref(_layernorm(h, axis=-1), L0_ffn_Wq_pk, L0_ffn_pk_keys, L0_ffn_Wq, L0_ffn_keys_table, L0_ffn_values_table, L0_ffn_Wo)
    return h

_drawn_inputs = setup_inputs


def setup_inputs(seed=0):
    import zlib

    import numpy as np

    out = dict(_drawn_inputs(seed))
    spreads = {}
    factors = {'L0_tok_proj_b': 4.573,
     'L0_ffn_Wq_pk': 64.0,
     'L0_ffn_pk_keys': 64.0,
     'L0_ffn_Wq': 64.0,
     'L0_ffn_keys_table': 64.0,
     'L0_ffn_values_table': 64.0,
     'L0_ffn_Wo': 64.0}
    for name, (base, spread) in spreads.items():
        noise = np.random.default_rng([zlib.crc32(name.encode()), seed]).standard_normal(out[name].shape)
        drawn = base * np.exp(spread * noise) if base else spread * noise
        out[name] = jnp.asarray(drawn.astype(out[name].dtype))
    for name, factor in factors.items():
        out[name] = (out[name] * factor).astype(out[name].dtype)
    return out
```

```python
import math
from contextlib import ExitStack

import numpy as np

import concourse.bass as bass
from concourse import mybir

F32 = mybir.dt.float32
BF16 = mybir.dt.bfloat16
I32 = mybir.dt.int32
U32 = mybir.dt.uint32
ALU = mybir.AluOpType
ACT = mybir.ActivationFunctionType
AX = mybir.AxisListType.X

P = 128
BANK = 512
BLK = BANK // P
EPS = 1e-5
LOWEST = -3.0e38
TOPK = 16
RSQRT_SEED = 0x5F3759DF
ROUND = 1.5 * 2.0**23


def two_pi_parts():
    c1 = np.float32(6.28125)
    c2 = np.float32(np.floor((2 * math.pi - float(c1)) * 2.0**26) / 2.0**26)
    c3 = np.float32(2 * math.pi - float(c1) - float(c2))
    return float(c1), float(c2), float(c3)


def staircase():
    runs, at = [], 0
    for a in range(TOPK):
        n = TOPK // (a + 1)
        if runs and runs[-1][2] == n:
            runs[-1][1] += 1
        else:
            runs.append([a, 1, n, at])
        at += n
    return runs, at


def lm_block(nc, x, a_n, b_n, rule_transform, token_rules, proj_w, proj_b, key_m, query_m, vin_m,
             vout_m, wq_pk, pk_keys, wq, keys_table, values_table, wo, out):
    NB, S = x.shape
    T = S // P
    VOCAB, D = a_n.shape
    H = key_m.shape[0]
    PAIRS = H // 2
    NRULES = rule_transform.shape[0]
    RC = NRULES // 2
    MG = 5
    RG = RC // MG
    NKEYS = pk_keys.shape[1]
    ROWS = keys_table.shape[0]
    HROWS = ROWS // H
    NP = 2 * H
    RUNS, NC = staircase()
    SLOTS = 5
    EQH = 2
    assert D == 64 and NKEYS == D and NRULES % (2 * MG) == 0

    kv_table = nc.dram_tensor("kv_table", [ROWS, 2 * D], F32, kind="Internal").ap()

    order = [(1, 0)]
    for i in range(T):
        order += [(2, i - 1)] * (i > 0) + [(1, i + 1)] * (i + 1 < T)
    order.append((2, T - 1))
    n_chunks = lambda t: (t + BLK) // BLK
    first_chunk, first_head, CHUNKS = {}, {}, 0
    for n, at in enumerate(order):
        first_chunk[at], first_head[at] = CHUNKS, n * H
        CHUNKS += H * n_chunks(at[1])
    HEADS = H * len(order)
    done_before = lambda att, t: sum(1 for o in order[: order.index((att, t))])

    with ExitStack() as ctx:
        def sb(name, shape, dt=F32):
            return ctx.enter_context(nc.sbuf_tensor(name, shape, dt))

        def sem(name):
            return ctx.enter_context(nc.semaphore(name))

        k2T = sb("k2T", [P, PAIRS, S])
        v2 = sb("v2", [P, T, H, D + 1])
        x1T = sb("x1T", [P, S])
        x1 = sb("x1", [P, T, D + 1])
        fourier = sb("fourier", [P, T, D])
        rule_of = sb("rule_of", [P, T])
        ids = sb("ids", [P, T], I32)
        rule_i = sb("rule_i", [P, T], I32)
        rules = sb("rules", [P, RC, D])
        M1 = sb("M1", [D, H * D])
        W1 = sb("W1", [P, PAIRS, D])
        W2 = sb("W2", [P, PAIRS, D])
        A = sb("A", [D, NP * NKEYS])
        Wq = sb("Wq", [D, H * D])
        projT = sb("projT", [D, 2 * D])
        projb = sb("projb", [P, 1])
        ident = sb("ident", [P, P])
        ident_bf = sb("ident_bf", [P, P], BF16)
        mask = sb("mask", [P, P], BF16)
        half = sb("half", [P, 1])
        head_row = sb("head_row", [P, H, TOPK])
        place = sb("place", [P, NC])
        freq = sb("freq", [P, D])
        angular = sb("angular", [P, D])
        fT = sb("fT", [D, P])
        base2 = sb("base2", [P, P])
        rule_row = sb("rule_row", [P, P])
        masked = sb("masked", [P, 2, MG, P])
        h0 = sb("h0", [P, D])
        h1 = sb("h1", [P, 4, D])
        stats = sb("stats", [P, 6])
        meanvar = sb("meanvar", [P, 2])
        rs = sb("rs", [P, 4])
        xd = sb("xd", [P, 2, D])
        x2 = sb("x2", [P, D])
        x2T = sb("x2T", [D, P])
        qT1 = sb("qT1", [P, PAIRS, P])
        qT2 = sb("qT2", [P, 2, PAIRS, P])
        work = sb("work", [P, EQH * TOPK * NC])
        sv = sb("sv", [P, NP, TOPK])
        si = sb("si", [P, NP, TOPK], U32)
        jrow = sb("jrow", [P, H, TOPK])
        cand = sb("cand", [P, H, NC])
        cand_row = sb("cand_row", [P, H, NC])
        fv = sb("fv", [P, H, TOPK])
        fpos = sb("fpos", [P, H, TOPK], U32)
        row_f = sb("row_f", [P, H, TOPK])
        wsum = sb("wsum", [P, H])
        weight = sb("weight", [P, 2, H, TOPK])
        row_u = sb("row_u", [P, 2, H * TOPK], U32)
        G = sb("G", [P, SLOTS, TOPK, 2 * D])
        kv = sb("kv", [P, 2, H, D])
        probs = sb("probs", [P, 4, BANK])
        probsT = sb("probsT", [P, 2, BANK])
        mx = sb("mx", [P, 2, 4])
        nmax = sb("nmax", [P, H])
        rec = sb("rec", [P, 2])
        Z = sb("Z", [P, H * D])
        ZT = sb("ZT", [P, PAIRS, P])
        obuf = sb("obuf", [P, 2, D])

        bank = [ctx.enter_context(nc.psum_tensor(f"bank{i}", [P, BANK], F32)) for i in range(8)]
        SB, TB, VB = bank[0:4], bank[4:6], bank[6:8]

        scores_pk = work[:, 0:NP * NKEYS].rearrange("p (n k) -> p n k", k=NKEYS)
        raw = lambda n, width: k2T[0:D, n // 4, (n % 4) * 512:(n % 4) * 512 + width]
        rawK, rawQ, rawVin, rawVout, rawWpk, rawPk, rawProj = (raw(n, 512) for n in range(7))
        flat = lambda n: k2T[:, 2 + n // 4, (n % 4) * 512:(n % 4) * 512 + 512]
        KT, QT, VinT = (k2T[0:D, 2, n * 512:(n + 1) * 512] for n in range(3))
        WpkT = k2T[:, 2, 1536:1536 + 256].rearrange("p (c e) -> p c e", e=D)
        pkD = k2T[:, 3, 0:1024].rearrange("p (c k) -> p c k", c=4)
        wide = lambda n: k2T[:, n // 2, (n % 2) * T * D:(n % 2 + 1) * T * D].rearrange("p (t f) -> p t f", f=D)
        e_a = G[:, 0, :, :].rearrange("p r d -> p (r d)")[:, 0:T * D].rearrange("p (t f) -> p t f", f=D)
        e_b = G[:, 1, :, :].rearrange("p r d -> p (r d)")[:, 0:T * D].rearrange("p (t f) -> p t f", f=D)
        idf = G[:, 2, 0:8, :].rearrange("p r d -> p (r d)")[:, 0:8 * T].rearrange("p (n t) -> p n t", t=T)

        s_wload = sem("weights_loaded"); s_table = sem("table_merged"); s_rules = sem("rules_loaded")
        s_const = sem("constants_made"); s_zero = sem("zeros_made"); s_pool = sem("pool_step")
        s_wT = sem("weights_transposed"); s_wTs = sem("weights_transposed_in_sbuf")
        s_wP = sem("weight_products"); s_wPs = sem("weight_products_in_sbuf")
        s_ids = sem("ids_loaded"); s_emb = [sem(f"embedding_gathered{n}") for n in range(3)]
        s_dve = sem("vector_step")
        s_angle = sem("angles"); s_trig = sem("sin_cos"); s_four = sem("fourier_ready")
        s_fT = sem("fourier_transposed"); s_fTs = sem("fourier_transposed_in_sbuf")
        s_base = sem("base_and_rule"); s_bases = sem("base_and_rule_in_sbuf")
        s_mask = sem("masked_ready"); s_ruled = sem("masked_used"); s_h0 = sem("h0_ready")
        s_xd = sem("x1_ready"); s_xT = sem("x1_transposed"); s_xTs = sem("x1T_in_sbuf")
        s_q1 = sem("q1"); s_q1s = sem("q1_in_sbuf")
        s_qk = sem("scores_ready"); s_max = sem("max_ready"); s_exp = sem("probs_ready")
        s_tr = sem("probs_transposed"); s_pt = sem("probsT_in_sbuf"); s_pv = sem("pv_done")
        s_norm = sem("head_normed")
        s_zT = sem("z_transposed"); s_zTs = sem("zT_in_sbuf"); s_proj = sem("attention_projected")
        s_h = sem("residual_added")
        s_x2 = sem("x2_ready"); s_x2T = sem("x2_transposed"); s_x2Ts = sem("x2T_in_sbuf")
        s_sim = sem("pk_scores"); s_sims = sem("pk_scores_in_sbuf")
        s_q2 = sem("q2"); s_q2s = sem("q2_in_sbuf")
        s_fd = sem("final_less_max"); s_fe = sem("final_exp")
        s_row = sem("rows_chosen")
        s_g = [sem(f"gathered{n}") for n in range(SLOTS)]
        s_comb = sem("head_combined")
        s_kT = sem("k_transposed"); s_kTs = sem("kT_in_sbuf"); s_vs = sem("v_in_sbuf")
        s_out = [sem(f"stored{n}") for n in range(2)]


        batch_sems = range(s_ids.num, s_out[-1].num + 1)

        def proj_after(att, t):
            return done_before(att, t) + 1

        with nc.Block() as setup:

            @setup.sync
            def _(sp):
                def load(dst, src):
                    sp.dma_start(dst, src).then_inc(s_wload, 16)

                load(rawK.rearrange("e (n d) -> e n d", d=D), key_m.rearrange("n e d -> e n d"))
                load(rawQ.rearrange("e (n d) -> e n d", d=D), query_m.rearrange("n e d -> e n d"))
                load(rawVin.rearrange("e (n d) -> e n d", d=D), vin_m.rearrange("n p d -> p n d"))
                load(rawVout.rearrange("e (n d) -> e n d", d=D), vout_m.rearrange("n d e -> d n e"))
                load(rawWpk, wq_pk)
                load(rawPk.rearrange("k (p c) -> k p c", p=2), pk_keys.rearrange("p k h d -> k p (h d)"))
                load(rawProj[:, 0:D], proj_w)
                load(Wq[:], wq)
                load(W2[:], wo.rearrange("(c q) e -> q c e", q=P))
                for r in range(2):
                    load(projb[r * D:(r + 1) * D, :], proj_b.unsqueeze(1))
                for r in range(2):
                    sp.dma_start(rules[r * D:(r + 1) * D, :, :],
                                 rule_transform.rearrange("(c r) d e -> r d c e", r=2)[r]).then_inc(s_rules, 16)


            @setup.gpsimd
            def _(pool):
                steps = [0]

                def step(ins):
                    steps[0] += 1
                    ins.then_inc(s_pool, 1)
                    pool.wait_ge(s_pool, steps[0])

                step(nc.gpsimd.memset(ident[:], 0.0))
                step(nc.gpsimd.affine_select(out=ident[:], in_=ident[:], compare_op=ALU.not_equal, fill=1.0,
                                             base=0, pattern=[[-1, P]], channel_multiplier=1))
                step(nc.gpsimd.tensor_copy(ident_bf[:], ident[:]))
                step(nc.gpsimd.memset(mask[:], 0.0))
                step(nc.gpsimd.affine_select(out=mask[:], in_=mask[:], compare_op=ALU.is_ge, fill=LOWEST,
                                             base=0, pattern=[[-1, P]], channel_multiplier=1))
                step(nc.gpsimd.memset(half[0:D, :], 0.0))
                step(nc.gpsimd.memset(half[D:P, :], -1.0))
                nc.gpsimd.iota(head_row[:], pattern=[[HROWS, H], [0, TOPK]], base=0, channel_multiplier=0,
                               allow_small_or_imprecise_dtypes=True)
                nc.gpsimd.iota(place[:], pattern=[[1, NC]], base=0, channel_multiplier=0,
                               allow_small_or_imprecise_dtypes=True)
                nc.gpsimd.iota(freq[:], pattern=[[1, D]], base=1, channel_multiplier=0,
                               allow_small_or_imprecise_dtypes=True).then_inc(s_const, 1)


            @setup.scalar
            def _(act):
                act.dma_start(kv_table[:, 0:D], keys_table).then_inc(s_table, 16)
                act.dma_start(kv_table[:, D:2 * D], values_table).then_inc(s_table, 16)

                act.wait_ge(s_wT, 1)
                act.wait_ge(s_zero, 1)
                for dst, src in ((KT, SB[0]), (QT, SB[1]), (VinT, SB[2])):
                    nc.scalar.copy(dst, src[0:D, :])
                nc.scalar.copy(WpkT, SB[3][:, 0:256].rearrange("p (c e) -> p c e", e=D))
                for c in range(4):
                    for r in range(4):
                        nc.scalar.copy(pkD[32 * r:32 * r + 32, c, D * r:D * r + D],
                                       SB[3][32 * r:32 * r + 32, 256 + D * c:256 + D * c + D])
                for r in range(2):
                    last = nc.scalar.copy(projT[:, r * D:(r + 1) * D], TB[0][0:D, 0:D])
                last.then_inc(s_wTs, 1)
                act.wait_ge(s_wP, 1)
                nc.scalar.copy(M1[:], SB[0][0:D, :])
                two = SB[1][0:D, :].rearrange("p (c r e) -> p c r e", r=2, e=D)
                for r in range(2):
                    nc.scalar.copy(W1[r * D:(r + 1) * D, :, :], two[:, :, r, :])
                for n in range(2):
                    last = nc.scalar.copy(A[:, n * 512:(n + 1) * 512], SB[2 + n][0:D, :])
                last.then_inc(s_wPs, 1)


            @setup.tensor
            def _(pe):
                pe.wait_ge(s_wload, 16 * 11)
                pe.wait_ge(s_const, 1)
                i64 = ident[0:D, 0:D]
                for n in range(H):
                    c = slice(n * D, (n + 1) * D)
                    nc.tensor.transpose(SB[0][0:D, c], rawK[:, c], i64)
                    nc.tensor.transpose(SB[1][0:D, c], rawQ[:, c], i64)
                    nc.tensor.transpose(SB[2][0:D, c], rawVin[:, c], i64)
                for c in range(4):
                    nc.tensor.transpose(SB[3][:, c * D:(c + 1) * D], rawWpk[:, c * P:(c + 1) * P], i64)
                    nc.tensor.transpose(SB[3][:, 256 + c * D:256 + (c + 1) * D], rawPk[:, c * P:(c + 1) * P], i64)
                nc.tensor.transpose(TB[0][0:D, 0:D], rawProj[:, 0:D], i64).then_inc(s_wT, 1)
                pe.wait_ge(s_wTs, 1)
                for n in range(H):
                    c = slice(n * D, (n + 1) * D)
                    nc.tensor.matmul(SB[0][0:D, c], KT[:, c], QT[:, c], start=True, stop=True)
                    nc.tensor.matmul(SB[1][0:D, c], VinT[:, c], rawVout[:, c], start=True, stop=True)
                for c in range(4):
                    last = nc.tensor.matmul(SB[2 + c // 2][0:D, (c % 2) * 256:(c % 2 + 1) * 256], WpkT[:, c, :],
                                            pkD[:, c, :], start=True, stop=True)
                last.then_inc(s_wP, 1)
                pe.wait_ge(s_wPs, 1)
                pe.wait_ge(s_rules, 32)


            @setup.vector
            def _(dve):
                nc.vector.memset(pkD, 0.0).then_inc(s_zero, 1)
                nc.vector.memset(x1[:, :, D:D + 1], 1.0)
                nc.vector.memset(v2[:, :, :, D:D + 1], 1.0)


        def batch(b):
            with nc.Block() as block:
                @block.sync
                def _(sp):
                    x_tiles = x.rearrange("b (t p) -> b p t", p=P)
                    out_tiles = out.rearrange("b (t p) e -> b t p e", p=P)
                    with nc.allow_non_contiguous_dma(reason="one id for each partition"):
                        sp.dma_start(ids[:], x_tiles[bass.ds(b, 1), :, :].rearrange("o p t -> p (o t)")).then_inc(s_ids, 16)
                    for t in range(T):
                        sp.wait_ge(s_h, proj_after(2, t))
                        sp.dma_start(out_tiles[bass.ds(b, 1), t, :, :].rearrange("o p e -> p (o e)"),
                                     obuf[:, t % 2, :]).then_inc(s_out[t % 2], 16)
                    for n in range(2):
                        sp.wait_ge(s_out[n], 16 * T // 2)

                @block.gpsimd
                def _(pool):
                    pool.wait_ge(s_ids, 16)
                    for t in range(T):
                        at = bass.IndirectOffsetOnAxis(ap=ids[:, t:t + 1].bitcast(U32), axis=0)
                        pool.indirect_dma_start(e_a[:, t, :], None, a_n, at).then_inc(s_emb[0], 16)
                        pool.indirect_dma_start(e_b[:, t, :], None, b_n, at).then_inc(s_emb[1], 16)
                        pool.indirect_dma_start(rule_i[:, t:t + 1], None, token_rules.unsqueeze(1), at).then_inc(s_emb[2], 16)
                    pool.wait_ge(s_table, 32)
                    pool.wait_ge(s_four, 1)
                    for t in range(T):
                        pool.wait_ge(s_row, t + 1)
                        for h in range(H):
                            n = t * H + h
                            if n >= SLOTS:
                                pool.wait_ge(s_comb, n - SLOTS + 1)
                            for r in range(TOPK):
                                c = h * TOPK + r
                                pool.indirect_dma_start(
                                    G[:, n % SLOTS, r, :], None, kv_table,
                                    bass.IndirectOffsetOnAxis(ap=row_u[:, t % 2, c:c + 1], axis=0),
                                ).then_inc(s_g[n % SLOTS], 16)
                    for n in range(3):
                        pool.wait_ge(s_emb[n], 16 * T)
                    for slot in range(SLOTS):
                        pool.wait_ge(s_g[slot], 16 * TOPK * len(range(slot, T * H, SLOTS)))
                    nc.gpsimd.dma_reset(batch_sems)

                @block.scalar
                def _(act):
                    def attention(att, t):
                        g0, n0, n = first_chunk[att, t], first_head[att, t], n_chunks(t)

                        def copy_probsT(g, width):
                            act.wait_ge(s_tr, g + 1)
                            if g >= 2:
                                act.wait_ge(s_pv, g - 1)
                            nc.scalar.copy(probsT[:, g % 2, 0:width], TB[g % 2][:, 0:width]).then_inc(s_pt, 1)

                        widths = [min(BLK, t + 1 - BLK * c) * P for c in range(n)]
                        for k in range(H * n):
                            h, c, g = k // n, k % n, g0 + k
                            if c == 0:
                                act.wait_ge(s_max, n0 + h + 1)
                            if g >= 4:
                                act.wait_ge(s_tr, g - 3)
                            nc.scalar.activation(probs[:, g % 4, 0:widths[c]], SB[g % 4][:, 0:widths[c]], ACT.Exp,
                                                 bias=nmax[:, h:h + 1]).then_inc(s_exp, 1)
                            if k:
                                copy_probsT(g - 1, widths[(k - 1) % n])
                        copy_probsT(g0 + H * n - 1, widths[-1])
                        act.wait_ge(s_zT, proj_after(att, t))
                        nc.scalar.copy(ZT[:], TB[0][:, :].rearrange("p (c q) -> p c q", q=P)).then_inc(s_zTs, 1)

                    def front(t):
                        done = t + 1
                        act.wait_ge(s_fT, done)
                        nc.scalar.copy(fT[:], VB[0][0:D, 0:P]).then_inc(s_fTs, 1)
                        act.wait_ge(s_base, done)
                        if t:
                            act.wait_ge(s_mask, t * RG)
                        nc.scalar.activation(base2[:], VB[1][:, 0:P], ACT.Identity, bias=projb[:, 0:1])
                        nc.scalar.activation(rule_row[:], VB[1][:, P:2 * P], ACT.Identity, bias=half[:, 0:1]).then_inc(s_bases, 1)
                        act.wait_ge(s_xT, done)
                        nc.scalar.copy(x1T[:, t * P:(t + 1) * P], VB[1][:, 0:P]).then_inc(s_xTs, 1)
                        act.wait_ge(s_q1, done)
                        nc.scalar.copy(qT1[:], VB[0][:, :].rearrange("p (c q) -> p c q", q=P)).then_inc(s_q1s, 1)
                        attention(1, t)
                        act.wait_ge(s_x2T, done)
                        nc.scalar.copy(x2T[:], VB[0][0:D, 0:P]).then_inc(s_x2Ts, 1)
                        act.wait_ge(s_sim, done)
                        if t:
                            act.wait_ge(s_row, t)
                        for n in range(2):
                            last = nc.scalar.copy(work[:, n * BANK:(n + 1) * BANK], SB[n][:, :])
                        last.then_inc(s_sims, 1)
                        act.wait_ge(s_q2, done)
                        nc.scalar.mul(qT2[:, t % 2, :, :], VB[1][:, :].rearrange("p (c q) -> p c q", q=P),
                                      float(D) ** -0.5).then_inc(s_q2s, 1)
                        act.wait_ge(s_fd, done)
                        nc.scalar.activation(weight[:, t % 2, :, :], weight[:, t % 2, :, :], ACT.Exp).then_inc(s_fe, 1)

                    def back(t):
                        act.wait_ge(s_comb, (t + 1) * H)
                        nc.scalar.copy(v2[:, t, :, 0:D], kv[:, 1, :, :]).then_inc(s_vs, 1)
                        act.wait_ge(s_kT, t + 1)
                        nc.scalar.copy(k2T[:, :, t * P:(t + 1) * P],
                                       TB[0][:, :].rearrange("p (c q) -> p c q", q=P)).then_inc(s_kTs, 1)
                        attention(2, t)

                    act.wait_ge(s_angle, 1)
                    nc.scalar.activation(wide(2), wide(2), ACT.Sin)
                    nc.scalar.activation(wide(3), wide(3), ACT.Sin).then_inc(s_trig, 1)
                    front(0)
                    for i in range(T):
                        if i > 0:
                            back(i - 1)
                        if i + 1 < T:
                            front(i + 1)
                    back(T - 1)

                @block.tensor
                def _(pe):
                    def attention(att, t):
                        g0, n0, n = first_chunk[att, t], first_head[att, t], n_chunks(t)
                        blocks = [min(BLK, t + 1 - BLK * c) for c in range(n)]
                        total = H * n

                        def scores(k):
                            h, c, g = k // n, k % n, g0 + k
                            rows = slice((h % 2) * D, (h % 2 + 1) * D)
                            if g >= 4:
                                pe.wait_ge(s_exp, g - 3)
                            keys = slice(c * BANK, c * BANK + blocks[c] * P)
                            q = (qT1 if att == 1 else qT2[:, t % 2, :, :])[rows, h // 2, :]
                            k_all = x1T[rows, keys] if att == 1 else k2T[rows, h // 2, keys]
                            diagonal = c == n - 1
                            last = nc.tensor.matmul(SB[g % 4][:, 0:blocks[c] * P], q, k_all, start=True, stop=not diagonal)
                            if diagonal:
                                last = nc.tensor.matmul(SB[g % 4][:, (blocks[c] - 1) * P:blocks[c] * P], ident_bf[:],
                                                        mask[:], start=False, stop=True)
                            last.then_inc(s_qk, 1)

                        def transposes(k):
                            g = g0 + k
                            pe.wait_ge(s_exp, g + 1)
                            if g >= 2:
                                pe.wait_ge(s_pt, g - 1)
                            for j in range(blocks[k % n]):
                                last = nc.tensor.transpose(TB[g % 2][:, j * P:(j + 1) * P],
                                                           probs[:, g % 4, j * P:(j + 1) * P], ident[:])
                            last.then_inc(s_tr, 1)

                        def weigh_values(k):
                            h, c, g = k // n, k % n, g0 + k
                            pe.wait_ge(s_pt, g + 1)
                            if c == 0 and n0 + h >= 2:
                                pe.wait_ge(s_norm, n0 + h - 1)
                            for j in range(blocks[c]):
                                at = c * BLK + j
                                v = x1[:, at, :] if att == 1 else v2[:, at, h, :]
                                last = nc.tensor.matmul(VB[h % 2][:, 0:D + 1], probsT[:, g % 2, j * P:(j + 1) * P], v,
                                                        start=at == 0, stop=at == t)
                            last.then_inc(s_pv, 1)

                        for k in range(min(4, total)):
                            scores(k)
                        for k in range(total):
                            transposes(k)
                            if k + 4 < total:
                                scores(k + 4)
                            if k:
                                weigh_values(k - 1)
                        weigh_values(total - 1)
                        pe.wait_ge(s_norm, n0 + H)
                        for c in range(PAIRS):
                            last = nc.tensor.transpose(TB[0][:, c * P:(c + 1) * P], Z[:, c * P:(c + 1) * P], ident[:])
                        last.then_inc(s_zT, 1)
                        done = proj_after(att, t)
                        pe.wait_ge(s_zTs, done)
                        w = W1 if att == 1 else W2
                        for c in range(PAIRS):
                            last = nc.tensor.matmul(TB[1][:, 0:D], ZT[:, c, :], w[:, c, :], start=c == 0, stop=c == PAIRS - 1)
                        last.then_inc(s_proj, 1)
                        pe.wait_ge(s_h, done)

                    def front(t):
                        done = t + 1
                        if t == 0:
                            pe.wait_ge(s_four, 1)
                        nc.tensor.transpose(VB[0][0:D, 0:P], fourier[:, t, :], ident[:]).then_inc(s_fT, 1)
                        pe.wait_ge(s_fTs, done)
                        nc.tensor.matmul(VB[1][:, 0:P], projT[:], fT[:], start=True, stop=True)
                        nc.tensor.matmul(VB[1][:, P:2 * P], rule_of[:, t:t + 1].to_broadcast([P, P]), ident[:],
                                         start=True, stop=True).then_inc(s_base, 1)
                        for g in range(RG):
                            pe.wait_ge(s_mask, t * RG + g + 1)
                            for j in range(MG):
                                c = g * MG + j
                                last = nc.tensor.matmul(VB[0][:, 0:D], masked[:, g % 2, j, :], rules[:, c, :],
                                                        start=c == 0, stop=c == RC - 1)
                            last.then_inc(s_ruled, 1)
                        pe.wait_ge(s_xd, done)
                        nc.tensor.transpose(VB[1][:, 0:P], xd[:].rearrange("p r f -> p (r f)"), ident[:]).then_inc(s_xT, 1)
                        pe.wait_ge(s_xTs, done)
                        for c in range(PAIRS):
                            last = nc.tensor.matmul(VB[0][:, c * P:(c + 1) * P], M1[:, c * P:(c + 1) * P],
                                                    x1T[0:D, t * P:(t + 1) * P], start=True, stop=True)
                        last.then_inc(s_q1, 1)
                        pe.wait_ge(s_q1s, done)
                        attention(1, t)
                        pe.wait_ge(s_x2, done)
                        nc.tensor.transpose(VB[0][0:D, 0:P], x2[:], ident[:]).then_inc(s_x2T, 1)
                        pe.wait_ge(s_x2Ts, done)
                        for n in range(2):
                            last = nc.tensor.matmul(SB[n][:, :], x2T[:], A[:, n * BANK:(n + 1) * BANK], start=True, stop=True)
                        last.then_inc(s_sim, 1)
                        for c in range(PAIRS):
                            last = nc.tensor.matmul(VB[1][:, c * P:(c + 1) * P], Wq[:, c * P:(c + 1) * P], x2T[:],
                                                    start=True, stop=True)
                        last.then_inc(s_q2, 1)
                        pe.wait_ge(s_sims, done)
                        pe.wait_ge(s_q2s, done)

                    def back(t):
                        pe.wait_ge(s_comb, (t + 1) * H)
                        for c in range(PAIRS):
                            last = nc.tensor.transpose(TB[0][:, c * P:(c + 1) * P],
                                                       kv[:, 0, 2 * c:2 * c + 2, :].rearrange("p h f -> p (h f)"), ident[:])
                        last.then_inc(s_kT, 1)
                        pe.wait_ge(s_kTs, t + 1)
                        pe.wait_ge(s_vs, t + 1)
                        attention(2, t)

                    front(0)
                    for i in range(T):
                        if i > 0:
                            back(i - 1)
                        if i + 1 < T:
                            front(i + 1)
                    back(T - 1)

                @block.vector
                def _(dve):
                    c1, c2, c3 = two_pi_parts()
                    steps = [0]
                    LN_STEPS = 14
                    EMB_STEPS = 21
                    TOP_STEPS = 14 + 3 * H // EQH
                    STEPS = (EMB_STEPS + T * (2 * LN_STEPS + TOP_STEPS) + T * H * (TOPK - 1)
                             + sum(H * (1 + (n_chunks(t) > 1)) for _, t in order))

                    def link(ins):
                        steps[0] += 1
                        ins.then_inc(s_dve, 1)
                        dve.wait_ge(s_dve, steps[0])

                    V = nc.vector

                    def embed():
                        dve.wait_ge(s_ids, 16)
                        f, r0, qa, qb, r = (idf[:, n, :] for n in range(5))
                        inv = float(np.float32(1.0) / np.float32(VOCAB))
                        link(V.tensor_copy(f, ids[:]))
                        link(V.tensor_scalar(r0, f, inv, None, ALU.mult))
                        link(V.tensor_scalar(qa.bitcast(I32), r0.bitcast(I32), -4096, None, ALU.bitwise_and))
                        link(V.tensor_tensor(qb, r0, qa, ALU.subtract))
                        hi, lo = float(VOCAB // 256 * 256), float(VOCAB % 256)
                        link(V.scalar_tensor_tensor(r, qa, -hi, f, ALU.mult, ALU.add))
                        link(V.scalar_tensor_tensor(r, qa, -lo, r, ALU.mult, ALU.add))
                        link(V.scalar_tensor_tensor(r, qb, -hi, r, ALU.mult, ALU.add))
                        link(V.scalar_tensor_tensor(r, qb, -lo, r, ALU.mult, ALU.add))
                        link(V.scalar_tensor_tensor(r0, r, inv, r0, ALU.mult, ALU.add))
                        shape = [P, T, D]
                        ang, k, sn, cs = (wide(n) for n in range(4))
                        link(V.tensor_scalar(angular[:], freq[:], float(np.float32(2.0 * math.pi)), None, ALU.mult))
                        link(V.tensor_tensor(ang, angular[:].unsqueeze(1).to_broadcast(shape),
                                                r0.unsqueeze(2).to_broadcast(shape), ALU.mult))
                        link(V.tensor_scalar(k, ang, 1.0 / (2.0 * math.pi), ROUND, ALU.mult, ALU.add))
                        link(V.tensor_scalar(k, k, ROUND, None, ALU.subtract))
                        link(V.scalar_tensor_tensor(ang, k, -c1, ang, ALU.mult, ALU.add))
                        link(V.scalar_tensor_tensor(ang, k, -c2, ang, ALU.mult, ALU.add))
                        link(V.scalar_tensor_tensor(ang, k, -c3, ang, ALU.mult, ALU.add))
                        link(V.tensor_scalar(sn, ang, 3.1415925, -3.1415925, ALU.min, ALU.max))
                        link(V.scalar_tensor_tensor(cs, sn, -1.0, sn, ALU.mult, ALU.max))
                        V.tensor_scalar(cs, cs, -1.0, math.pi / 2, ALU.mult, ALU.add).then_inc(s_angle, 1)
                        dve.wait_ge(s_trig, 1)
                        for n in range(2):
                            dve.wait_ge(s_emb[n], 16 * T)
                        link(V.tensor_tensor(e_a, e_a, cs, ALU.mult))
                        link(V.tensor_tensor(e_b, e_b, sn, ALU.mult))
                        dve.wait_ge(s_emb[2], 16 * T)
                        link(V.tensor_copy(rule_of[:], rule_i[:]))
                        V.tensor_tensor(fourier[:], e_a, e_b, ALU.add).then_inc(s_four, 1)

                    def layernorm_scale(src):
                        v, y, u = rs[:, 0:1], rs[:, 1:2], rs[:, 2:3]
                        link(V.bn_stats(stats[:], src))
                        link(V.bn_aggr(meanvar[:], stats[:]))
                        link(V.tensor_scalar(v, meanvar[:, 1:2], EPS, None, ALU.add))
                        link(V.tensor_scalar(u.bitcast(I32), v.bitcast(I32), 1, None, ALU.logical_shift_right))
                        link(V.tensor_scalar(y.bitcast(I32), u.bitcast(I32), -1.0, float(RSQRT_SEED), ALU.mult, ALU.add))
                        for _ in range(3):
                            link(V.tensor_scalar(u, y, y, v, ALU.mult, ALU.mult))
                            link(V.tensor_scalar(u, u, -0.5, 1.5, ALU.mult, ALU.add))
                            link(V.tensor_tensor(y, y, u, ALU.mult))

                    def attention(att, t):
                        g0, n0, n = first_chunk[att, t], first_head[att, t], n_chunks(t)
                        widths = [min(BLK, t + 1 - BLK * c) * P for c in range(n)]

                        def norm(h):
                            dve.wait_ge(s_pv, g0 + (h + 1) * n)
                            o = VB[h % 2]
                            link(V.reciprocal(rec[:, h % 2:h % 2 + 1], o[:, D:D + 1]))
                            V.tensor_scalar(Z[:, h * D:(h + 1) * D], o[:, 0:D], rec[:, h % 2:h % 2 + 1], None,
                                            ALU.mult).then_inc(s_norm, 1)

                        for h in range(H):
                            for c in range(n):
                                g = g0 + h * n + c
                                dve.wait_ge(s_qk, g + 1)
                                dst = nmax[:, h:h + 1] if n == 1 else mx[:, h % 2, c:c + 1]
                                last = V.tensor_reduce(dst, SB[g % 4][:, 0:widths[c]], AX, ALU.max, negate=n == 1)
                            if n > 1:
                                link(last)
                                last = V.tensor_reduce(nmax[:, h:h + 1], mx[:, h % 2, 0:n], AX, ALU.max, negate=True)
                            last.then_inc(s_max, 1)
                            if h:
                                norm(h - 1)
                        norm(H - 1)
                        dve.wait_ge(s_proj, proj_after(att, t))

                    def top16(values, first, second, index, n):
                        for rank, place_ in ((slice(0, 8), 0), (slice(8, 16), 1)):
                            for j in range(n):
                                last = V.max(first[:, j, rank], values[:, j, :])
                            link(last)
                            for j in range(n):
                                last = V.max_index(index[:, j, rank], first[:, j, rank], values[:, j, :])
                            if place_ == 0:
                                for j in range(n):
                                    last = V.match_replace(values[:, j, :], first[:, j, rank], values[:, j, :], LOWEST)
                            link(last)

                    def front(t):
                        done = t + 1
                        dve.wait_ge(s_bases, done)
                        for g in range(RG):
                            n = t * RG + g
                            if t * RG + g >= 2:
                                dve.wait_ge(s_ruled, n - 1)
                            for j in range(MG):
                                last = V.scalar_tensor_tensor(masked[:, g % 2, j, :], rule_row[:], 2.0 * (g * MG + j),
                                                              base2[:], ALU.is_equal, ALU.mult)
                            last.then_inc(s_mask, 1)
                        dve.wait_ge(s_ruled, (t + 1) * RG)
                        link(V.tensor_copy(h0[:], VB[0][:, 0:D]))
                        layernorm_scale(h0[:])
                        V.tensor_scalar(xd[:], h0[:].unsqueeze(1).to_broadcast([P, 2, D]), meanvar[:, 0:1], rs[:, 1:2],
                                        ALU.subtract, ALU.mult)
                        V.tensor_scalar(x1[:, t, 0:D], h0[:], meanvar[:, 0:1], rs[:, 1:2],
                                        ALU.subtract, ALU.mult).then_inc(s_xd, 1)
                        attention(1, t)
                        h = h1[:, t % 4, :]
                        V.tensor_tensor(h, TB[1][:, 0:D], h0[:], ALU.add).then_inc(s_h, 1)
                        dve.wait_ge(s_h, proj_after(1, t))
                        layernorm_scale(h)
                        V.tensor_scalar(x2[:], h, meanvar[:, 0:1], rs[:, 1:2], ALU.subtract, ALU.mult).then_inc(s_x2, 1)

                        dve.wait_ge(s_sims, done)
                        top16(scores_pk, sv, None, si, NP)
                        s0, s1, i0, i1 = sv[:, 0:H, :], sv[:, H:NP, :], si[:, 0:H, :], si[:, H:NP, :]
                        link(V.scalar_tensor_tensor(jrow[:], i1, float(NKEYS), head_row[:], ALU.mult, ALU.add))
                        for a, rows, n, at in RUNS:
                            for dst, left, right in ((cand, s0, s1), (cand_row, i0, jrow)):
                                if rows == 1:
                                    o, l, r = (dst[:, :, at:at + n], left[:, :, a:a + 1].to_broadcast([P, H, n]),
                                               right[:, :, 0:n])
                                else:
                                    shape = [P, H, rows, n]
                                    o = dst[:, :, at:at + rows * n].rearrange("p h (a b) -> p h a b", b=n)
                                    l = left[:, :, a:a + rows].unsqueeze(3).to_broadcast(shape)
                                    r = right[:, :, 0:n].unsqueeze(2).to_broadcast(shape)
                                last = V.tensor_tensor(o, l, r, ALU.add)
                        link(last)
                        top16(cand, fv, None, fpos, H)
                        w = weight[:, t % 2, :, :]
                        V.tensor_tensor(w, fv[:], fv[:, :, 0:1].to_broadcast([P, H, TOPK]), ALU.subtract).then_inc(s_fd, 1)
                        for e in range(H // EQH):
                            hs = slice(e * EQH, (e + 1) * EQH)
                            eq = work[:].rearrange("p (h r c) -> p (h r) c", h=EQH, c=NC)
                            shape = [P, EQH * TOPK, NC]
                            link(V.tensor_tensor(eq, fpos[:, hs, :].rearrange("p h r -> p (h r)").unsqueeze(2).to_broadcast(shape),
                                                    place[:].unsqueeze(1).to_broadcast(shape), ALU.is_equal))
                            eq4 = work[:].rearrange("p (h r c) -> p h r c", h=EQH, c=NC)
                            link(V.tensor_tensor(eq4, eq4, cand_row[:, hs, :].unsqueeze(2).to_broadcast([P, EQH, TOPK, NC]),
                                                    ALU.mult))
                            link(V.tensor_reduce(row_f[:, hs, :].rearrange("p h r -> p (h r)"), eq, AX, ALU.add))
                        dve.wait_ge(s_fe, done)
                        link(V.tensor_reduce(wsum[:], w, AX, ALU.add))
                        link(V.reciprocal(wsum[:], wsum[:]))
                        link(V.tensor_tensor(w, w, wsum[:].unsqueeze(2).to_broadcast([P, H, TOPK]), ALU.mult))
                        V.tensor_copy(row_u[:, t % 2, :], row_f[:].rearrange("p h r -> p (h r)")).then_inc(s_row, 1)

                    def combine(t):
                        for h in range(H):
                            n = t * H + h
                            slot = n % SLOTS
                            uses = len(range(slot, T * H, SLOTS))
                            if h == 0 and t:
                                dve.wait_ge(s_kTs, t)
                                dve.wait_ge(s_vs, t)
                            dve.wait_ge(s_g[slot], 256 * (n // SLOTS + 1))
                            w = weight[:, t % 2, h, :]
                            acc = kv[:, :, h, :]
                            rows = G[:, slot, :, :].rearrange("p r (m f) -> p r m f", m=2)
                            for r in range(TOPK):
                                if r == 0:
                                    last = V.tensor_scalar(acc, rows[:, 0, :, :], w[:, 0:1], None, ALU.mult)
                                else:
                                    link(last)
                                    last = V.scalar_tensor_tensor(acc, rows[:, r, :, :], w[:, r:r + 1], acc, ALU.mult, ALU.add)
                            last.then_inc(s_comb, 1)

                    def back(t):
                        attention(2, t)
                        if t >= 2:
                            dve.wait_ge(s_out[t % 2], 16 * (t // 2))
                        V.tensor_tensor(obuf[:, t % 2, :], TB[1][:, 0:D], h1[:, t % 4, :], ALU.add).then_inc(s_h, 1)

                    embed()
                    front(0)
                    for i in range(T):
                        if i > 0:
                            back(i - 1)
                        if i + 1 < T:
                            front(i + 1)
                        combine(i)
                    back(T - 1)
                    assert steps[0] == STEPS, (steps[0], STEPS)


        with nc.Fori(0, NB) as b:
            batch(b)
            nc.all_engine_barrier(sems_to_clear=batch_sems)


_INS = ["x", "L0_tok_a_n", "L0_tok_b_n", "L0_tok_rule_transform", "L0_tok_token_rules", "L0_tok_proj_w",
        "L0_tok_proj_b", "L0_attn_key_matrices", "L0_attn_query_matrices", "L0_attn_value_in_matrices",
        "L0_attn_value_out_matrices", "L0_ffn_Wq_pk", "L0_ffn_pk_keys", "L0_ffn_Wq", "L0_ffn_keys_table",
        "L0_ffn_values_table", "L0_ffn_Wo"]


def kernel(**inputs):
    import numpy as _np
    import concourse.bacc as _bacc
    from concourse import mybir as _mybir
    from concourse.bass_utils import run_bass_kernel_spmd as _run

    nc = _bacc.Bacc("TRN2", target_bir_lowering=False, num_devices=1)
    arrays, args = {}, []
    for name in _INS:
        a = _np.ascontiguousarray(inputs[name])
        arrays[f"in_{name}"] = a
        args.append(nc.dram_tensor(f"in_{name}", a.shape, _mybir.dt.from_np(a.dtype), kind="ExternalInput").ap())
    b, s = inputs["x"].shape
    out = nc.dram_tensor("out_rows", (b, s, inputs["L0_tok_a_n"].shape[1]), _mybir.dt.float32, kind="ExternalOutput").ap()
    lm_block(nc, *args, out)
    r = _run(nc, [arrays], core_ids=[0])
    return r.results[0]["out_rows"]
```

```python
import math
from contextlib import ExitStack

import numpy as np

import concourse.bass as bass
from concourse import mybir

F32 = mybir.dt.float32
BF16 = mybir.dt.bfloat16
I32 = mybir.dt.int32
U32 = mybir.dt.uint32
ALU = mybir.AluOpType
ACT = mybir.ActivationFunctionType
AX = mybir.AxisListType.X

P = 128
BANK = 512
BLK = BANK // P
EPS = 1e-5
LOWEST = -3.0e38
TOPK = 16
RSQRT_SEED = 0x5F3759DF
ROUND = 1.5 * 2.0**23


def two_pi_parts():
    c1 = np.float32(6.28125)
    c2 = np.float32(np.floor((2 * math.pi - float(c1)) * 2.0**26) / 2.0**26)
    c3 = np.float32(2 * math.pi - float(c1) - float(c2))
    return float(c1), float(c2), float(c3)


def staircase():
    runs, at = [], 0
    for a in range(TOPK):
        n = TOPK // (a + 1)
        if runs and runs[-1][2] == n:
            runs[-1][1] += 1
        else:
            runs.append([a, 1, n, at])
        at += n
    return runs, at


def lm_block(nc, x, a_n, b_n, rule_transform, token_rules, proj_w, proj_b, key_m, query_m, vin_m,
             vout_m, wq_pk, pk_keys, wq, keys_table, values_table, wo, out):
    NB, S = x.shape
    T = S // P
    VOCAB, D = a_n.shape
    H = key_m.shape[0]
    PAIRS = H // 2
    NRULES = rule_transform.shape[0]
    RC = NRULES // 2
    MG = 5
    RG = RC // MG
    NKEYS = pk_keys.shape[1]
    ROWS = keys_table.shape[0]
    HROWS = ROWS // H
    NP = 2 * H
    RUNS, NC = staircase()
    SLOTS = 4
    EQH = 2
    LEAD = 3
    RING = LEAD + 1
    GT = 4
    CODE = 2 * ROWS
    assert CODE * NC < 2**24
    assert D == 64 and NKEYS == D and NRULES % (2 * MG) == 0

    kv_table = nc.dram_tensor("kv_table", [ROWS, 2 * D], F32, kind="Internal").ap()

    plan = []

    def plan_front(t):
        if t < T:
            if t % GT == 0:
                plan.append(("embed", t // GT))
            plan.append(("front", t))

    for t in range(LEAD):
        plan_front(t)
    for t in range(T):
        if t:
            plan.append(("back", t - 1))
        plan_front(t + LEAD)
    plan.append(("back", T - 1))

    heads_at = {}
    for t in range(T):
        if t == 0:
            places = [("front", LEAD, p) for p in ("normed", 0, 2, 4, 6, "added", "parts", "rows")]
        elif t + LEAD < T:
            places = ([("back", t - 1, p) for p in (0, 2, 4, 6)] +
                      [("front", t + LEAD, p) for p in ('normed', 2, 6, 'parts')])
        elif t < T - 1:
            places = [("back", t - 1, p) for p in (0, 1, 2, 3, 4, 5, 6, 7)]
        else:
            places = [("back", t - 1, p) for p in (0, 2, 4, 6)] + [("back", t, p) for p in (4, 4, 6, 6)]
        for h in range(H):
            heads_at.setdefault(places[h], []).append((t, h))

    order = [(1 if what == "front" else 2, t) for what, t in plan if what in ("front", "back")]
    n_chunks = lambda t: (t + BLK) // BLK
    first_chunk, first_head, CHUNKS = {}, {}, 0
    for n, at in enumerate(order):
        first_chunk[at], first_head[at] = CHUNKS, n * H
        CHUNKS += H * n_chunks(at[1])

    with ExitStack() as ctx:
        def sb(name, shape, dt=F32):
            return ctx.enter_context(nc.sbuf_tensor(name, shape, dt))

        def sem(name):
            return ctx.enter_context(nc.semaphore(name))

        k2T = sb("k2T", [P, PAIRS, S])
        v2 = sb("v2", [P, T, H, D + 1])
        x1T = sb("x1T", [P, S])
        x1 = sb("x1", [P, T, D + 1])
        e_a = sb("e_a", [P, 2, GT, D])
        e_b = sb("e_b", [P, 2, GT, D])
        quotient = sb("quotient", [P, T])
        rule_of = sb("rule_of", [P, T])
        ids = sb("ids", [P, T], I32)
        rule_i = sb("rule_i", [P, 2, GT], I32)
        rules = sb("rules", [P, RC, D])
        M1 = sb("M1", [P, H * D])
        WX1 = sb("WX1", [D + 1, H, D + 1])
        WX2 = sb("WX2", [D + 1, H, D + 1])
        A = sb("A", [P, NP * NKEYS])
        Wq = sb("Wq", [P, H * D])
        projT = sb("projT", [P, 2 * D])
        projb = sb("projb", [P, 1])
        ident = sb("ident", [P, P])
        ident_bf = sb("ident_bf", [P, P], BF16)
        mask = sb("mask", [P, P], BF16)
        half = sb("half", [P, 1])
        head_row = sb("head_row", [P, H, TOPK])
        place = sb("place", [P, NC])
        freq = sb("freq", [P, D])
        angular = sb("angular", [P, D])
        fT = sb("fT", [P, P])
        base2 = sb("base2", [P, P])
        rule_row = sb("rule_row", [P, P])
        masked = sb("masked", [P, 2, MG, P])
        h0 = sb("h0", [P, D])
        hT = sb("hT", [D, P])
        h1 = sb("h1", [P, RING, D])
        stats = sb("stats", [P, 6])
        meanvar = sb("meanvar", [P, 2])
        rs = sb("rs", [P, 4])
        xd = sb("xd", [P, 2, D])
        x2T = sb("x2T", [P, P])
        qT2 = sb("qT2", [P, RING, PAIRS, P])
        q1 = sb("q1", [P, H, P])
        q2 = sb("q2", [P, H, P])
        work = sb("work", [P, EQH * TOPK * NC])
        sv = sb("sv", [P, NP, TOPK])
        si = sb("si", [P, NP, TOPK], U32)
        jrow = sb("jrow", [P, H, TOPK])
        cand = sb("cand", [P, H, NC])
        cand_row = sb("cand_row", [P, H, NC])
        fv = sb("fv", [P, H, TOPK])
        fpos = sb("fpos", [P, H, TOPK], U32)
        fcode = sb("fcode", [P, H, TOPK])
        wsum = sb("wsum", [P, H])
        weight = sb("weight", [P, RING, H, TOPK])
        row_u = sb("row_u", [P, RING, H * TOPK], U32)
        G = sb("G", [P, SLOTS, TOPK, 2 * D])
        kv = sb("kv", [P, H, 2 * D])
        k_rows = sb("k_rows", [P, H * D])
        probs = sb("probs", [P, 4, BANK])
        probsT = sb("probsT", [P, 2, BANK])
        mx = sb("mx", [P, 2, 4])
        nmax = sb("nmax", [P, H])
        rec = sb("rec", [P, 2])
        zT = sb("zT", [D + 1, 2, P])
        obuf = sb("obuf", [P, 2, D])

        bank = [ctx.enter_context(nc.psum_tensor(f"bank{i}", [P, BANK], F32)) for i in range(8)]
        SB, TB, VB = bank[0:4], bank[4:6], bank[6:8]

        trig = masked[:].rearrange("p a b c -> p (a b c)")[:, 0:4 * GT * D].rearrange("p (n t f) -> p n t f", n=4, f=D)
        scores_pk = work[:, 0:NP * NKEYS].rearrange("p (n k) -> p n k", k=NKEYS)
        raw = lambda n, width: k2T[0:D, n // 4, (n % 4) * 512:(n % 4) * 512 + width]
        rawK, rawQ, rawVin, rawVout, rawWpk, rawPk, rawProj = (raw(n, 512) for n in range(7))
        KT, QT, VinT = (k2T[0:D, 2, n * 512:(n + 1) * 512] for n in range(3))
        WpkT = k2T[:, 2, 1536:1536 + 256].rearrange("p (c e) -> p c e", e=D)
        pkD = k2T[:, 3, 0:1024].rearrange("p (c k) -> p c k", c=4)

        s_wload = sem("weights_loaded"); s_table = sem("table_merged"); s_rules = sem("rules_loaded")
        s_const = sem("constants_made"); s_zero = sem("zeros_made"); s_cleared = sem("cleared"); s_pool = sem("pool_step")
        s_wT = sem("weights_transposed"); s_wTs = sem("weights_transposed_in_sbuf")
        s_wP = sem("weight_products"); s_wPs = sem("weight_products_in_sbuf")
        s_ids = sem("ids_loaded"); s_emb = [sem(f"embedding_gathered{n}") for n in range(2)]
        s_dve = sem("vector_step")
        s_angle = sem("angles"); s_trig = sem("sin_cos"); s_four = sem("fourier_ready")
        s_fT = sem("fourier_transposed"); s_fTs = sem("fourier_transposed_in_sbuf")
        s_base = sem("base_and_rule"); s_bases = sem("base_and_rule_in_sbuf")
        s_mask = sem("masked_ready"); s_ruled = sem("masked_used");
        s_xd = sem("x1_ready"); s_xT = sem("x1_transposed"); s_xTs = sem("x1T_in_sbuf")
        s_q1 = sem("q1"); s_q1s = sem("q1_in_sbuf")
        s_qk = sem("scores_ready"); s_max = sem("max_ready"); s_exp = sem("probs_ready")
        s_tr = sem("probs_transposed"); s_pt = sem("probsT_in_sbuf"); s_pv = sem("pv_done")
        s_zTs = sem("zT_in_sbuf"); s_y = sem("head_projected"); s_acc = sem("head_added")
        s_hTs = sem("hT_in_sbuf"); s_h0 = sem("h0_ready")
        s_q2p = sem("q2_padded")
        s_h = sem("residual_added")
        s_x2 = sem("x2_ready"); s_x2T = sem("x2_transposed"); s_x2Ts = sem("x2T_in_sbuf")
        s_sim = sem("pk_scores"); s_sims = sem("pk_scores_in_sbuf")
        s_q2 = sem("q2"); s_q2s = sem("q2_in_sbuf")
        s_fd = sem("final_less_max"); s_fe = sem("final_exp")
        s_row = sem("rows_chosen")
        s_g = [sem(f"gathered{n}") for n in range(SLOTS)]
        s_comb = sem("head_combined")
        s_ks = sem("k_rows_copied"); s_kT = sem("k_transposed"); s_kTs = sem("kT_in_sbuf"); s_vs = sem("v_in_sbuf")
        s_out = [sem(f"stored{n}") for n in range(2)]


        batch_sems = range(s_ids.num, s_out[-1].num + 1)

        with nc.Block() as setup:

            @setup.sync
            def _(sp):
                def load(dst, src):
                    sp.dma_start(dst, src).then_inc(s_wload, 16)

                load(rawK.rearrange("e (n d) -> e n d", d=D), key_m.rearrange("n e d -> e n d"))
                load(rawQ.rearrange("e (n d) -> e n d", d=D), query_m.rearrange("n e d -> e n d"))
                load(rawVin.rearrange("e (n d) -> e n d", d=D), vin_m.rearrange("n p d -> p n d"))
                load(rawVout.rearrange("e (n d) -> e n d", d=D), vout_m.rearrange("n d e -> d n e"))
                load(rawWpk, wq_pk)
                load(rawPk.rearrange("k (p c) -> k p c", p=2), pk_keys.rearrange("p k h d -> k p (h d)"))
                load(rawProj[:, 0:D], proj_w)
                load(Wq[0:D, :], wq)
                sp.wait_ge(s_zero, 1)
                load(WX2[0:D, :, 0:D], wo.rearrange("(h d) e -> d h e", h=H))
                for r in range(2):
                    load(projb[r * D:(r + 1) * D, :], proj_b.unsqueeze(1))
                for r in range(2):
                    sp.dma_start(rules[r * D:(r + 1) * D, :, :],
                                 rule_transform.rearrange("(c r) d e -> r d c e", r=2)[r]).then_inc(s_rules, 16)


            @setup.gpsimd
            def _(pool):
                steps = [0]

                def step(ins):
                    steps[0] += 1
                    ins.then_inc(s_pool, 1)
                    pool.wait_ge(s_pool, steps[0])

                step(nc.gpsimd.memset(ident[:], 0.0))
                step(nc.gpsimd.affine_select(out=ident[:], in_=ident[:], compare_op=ALU.not_equal, fill=1.0,
                                             base=0, pattern=[[-1, P]], channel_multiplier=1))
                step(nc.gpsimd.tensor_copy(ident_bf[:], ident[:]))
                step(nc.gpsimd.memset(mask[:], 0.0))
                step(nc.gpsimd.affine_select(out=mask[:], in_=mask[:], compare_op=ALU.is_ge, fill=LOWEST,
                                             base=0, pattern=[[-1, P]], channel_multiplier=1))
                step(nc.gpsimd.memset(half[0:D, :], 0.0))
                nc.gpsimd.iota(head_row[:], pattern=[[HROWS, H], [0, TOPK]], base=0, channel_multiplier=0,
                               allow_small_or_imprecise_dtypes=True)
                nc.gpsimd.iota(place[:], pattern=[[1, NC]], base=0, channel_multiplier=0,
                               allow_small_or_imprecise_dtypes=True)
                step(nc.gpsimd.iota(freq[:], pattern=[[1, D]], base=1, channel_multiplier=0,
                               allow_small_or_imprecise_dtypes=True))
                step(nc.gpsimd.tensor_scalar(place[:], place[:], float(CODE), None, ALU.mult))
                nc.gpsimd.memset(half[D:P, :], -1.0).then_inc(s_const, 1)


            @setup.scalar
            def _(act):
                act.dma_start(kv_table[:, 0:D], keys_table).then_inc(s_table, 16)
                act.dma_start(kv_table[:, D:2 * D], values_table).then_inc(s_table, 16)

                act.wait_ge(s_wT, 1)
                act.wait_ge(s_zero, 1)
                for dst, src in ((KT, SB[0]), (QT, SB[1]), (VinT, SB[2])):
                    nc.scalar.copy(dst, src[0:D, :])
                nc.scalar.copy(WpkT, SB[3][:, 0:256].rearrange("p (c e) -> p c e", e=D))
                for c in range(4):
                    for r in range(4):
                        nc.scalar.copy(pkD[32 * r:32 * r + 32, c, D * r:D * r + D],
                                       SB[3][32 * r:32 * r + 32, 256 + D * c:256 + D * c + D])
                for r in range(2):
                    last = nc.scalar.copy(projT[0:D, r * D:(r + 1) * D], TB[0][0:D, 0:D])
                last.then_inc(s_wTs, 1)
                act.wait_ge(s_wP, 1)
                nc.scalar.copy(M1[0:D, :], SB[0][0:D, :])
                nc.scalar.copy(WX1[0:D, :, 0:D], SB[1][0:D, :].rearrange("p (n e) -> p n e", e=D))
                for n in range(2):
                    last = nc.scalar.copy(A[0:D, n * 512:(n + 1) * 512], SB[2 + n][0:D, :])
                last.then_inc(s_wPs, 1)


            @setup.tensor
            def _(pe):
                pe.wait_ge(s_wload, 16 * 11)
                pe.wait_ge(s_const, 1)
                i64 = ident[0:D, 0:D]
                for n in range(H):
                    c = slice(n * D, (n + 1) * D)
                    nc.tensor.transpose(SB[0][0:D, c], rawK[:, c], i64)
                    nc.tensor.transpose(SB[1][0:D, c], rawQ[:, c], i64)
                    nc.tensor.transpose(SB[2][0:D, c], rawVin[:, c], i64)
                for c in range(4):
                    nc.tensor.transpose(SB[3][:, c * D:(c + 1) * D], rawWpk[:, c * P:(c + 1) * P], i64)
                    nc.tensor.transpose(SB[3][:, 256 + c * D:256 + (c + 1) * D], rawPk[:, c * P:(c + 1) * P], i64)
                nc.tensor.transpose(TB[0][0:D, 0:D], rawProj[:, 0:D], i64).then_inc(s_wT, 1)
                pe.wait_ge(s_wTs, 1)
                for n in range(H):
                    c = slice(n * D, (n + 1) * D)
                    nc.tensor.matmul(SB[0][0:D, c], KT[:, c], QT[:, c], start=True, stop=True)
                    nc.tensor.matmul(SB[1][0:D, c], VinT[:, c], rawVout[:, c], start=True, stop=True)
                for c in range(4):
                    last = nc.tensor.matmul(SB[2 + c // 2][0:D, (c % 2) * 256:(c % 2 + 1) * 256], WpkT[:, c, :],
                                            pkD[:, c, :], start=True, stop=True)
                last.then_inc(s_wP, 1)
                pe.wait_ge(s_wPs, 1)
                pe.wait_ge(s_rules, 32)


            @setup.vector
            def _(dve):
                for zero in (M1[D:P, :], A[D:P, :], Wq[D:P, :], projT[D:P, :], fT[D:P, :], q1[:], q2[:], WX1[:], WX2[:]):
                    last = nc.vector.memset(zero, 0.0)
                last.then_inc(s_cleared, 1)
                dve.wait_ge(s_cleared, 1)
                nc.vector.memset(WX1[D:D + 1, :, D:D + 1], 1.0)
                nc.vector.memset(WX2[D:D + 1, :, D:D + 1], 1.0)
                nc.vector.memset(pkD, 0.0).then_inc(s_zero, 1)
                nc.vector.memset(x1[:, :, D:D + 1], 1.0)
                nc.vector.memset(v2[:, :, :, D:D + 1], 1.0)


        def batch(b):
            with nc.Block() as block:
                @block.sync
                def _(sp):
                    x_tiles = x.rearrange("b (t p) -> b p t", p=P)
                    out_tiles = out.rearrange("b (t p) e -> b t p e", p=P)
                    with nc.allow_non_contiguous_dma(reason="one id for each partition"):
                        sp.dma_start(ids[:], x_tiles[bass.ds(b, 1), :, :].rearrange("o p t -> p (o t)")).then_inc(s_ids, 16)
                    for t in range(T):
                        sp.wait_ge(s_h, order.index((2, t)) + 1)
                        sp.dma_start(out_tiles[bass.ds(b, 1), t, :, :].rearrange("o p e -> p (o e)"),
                                     obuf[:, t % 2, :]).then_inc(s_out[t % 2], 16)
                    for n in range(2):
                        sp.wait_ge(s_out[n], 16 * T // 2)

                @block.gpsimd
                def _(pool):
                    def embedding(g):
                        if g >= 2:
                            pool.wait_ge(s_fT, GT * (g - 1))
                        for j in range(GT):
                            t = g * GT + j
                            at = bass.IndirectOffsetOnAxis(ap=ids[:, t:t + 1].bitcast(U32), axis=0)
                            e = g % 2
                            pool.indirect_dma_start(e_a[:, e, j, :], None, a_n, at).then_inc(s_emb[e], 16)
                            pool.indirect_dma_start(e_b[:, e, j, :], None, b_n, at).then_inc(s_emb[e], 16)
                            pool.indirect_dma_start(rule_i[:, e, j:j + 1], None, token_rules.unsqueeze(1), at).then_inc(s_emb[e], 16)

                    pool.wait_ge(s_ids, 16)
                    embedding(0)
                    embedding(1)
                    pool.wait_ge(s_table, 32)
                    for t in range(T):
                        g = (t + LEAD + 1) // GT
                        if (t + LEAD + 1) % GT == 0 and 2 <= g < T // GT:
                            embedding(g)
                        pool.wait_ge(s_row, t + 1)
                        for h in range(H):
                            n = t * H + h
                            if n >= SLOTS:
                                pool.wait_ge(s_comb, n - SLOTS + 1)
                            for r in range(TOPK):
                                c = h * TOPK + r
                                pool.indirect_dma_start(
                                    G[:, n % SLOTS, r, :], None, kv_table,
                                    bass.IndirectOffsetOnAxis(ap=row_u[:, t % RING, c:c + 1], axis=0),
                                ).then_inc(s_g[n % SLOTS], 16)
                    for e in range(2):
                        pool.wait_ge(s_emb[e], 16 * 3 * T // 2)
                    for slot in range(SLOTS):
                        pool.wait_ge(s_g[slot], 16 * TOPK * len(range(slot, T * H, SLOTS)))
                    nc.gpsimd.dma_reset(batch_sems)

                @block.scalar
                def _(act):
                    def attention(att, t):
                        g0, n0, n = first_chunk[att, t], first_head[att, t], n_chunks(t)
                        widths = [min(BLK, t + 1 - BLK * c) * P for c in range(n)]
                        total = H * n

                        def copy_probsT(k):
                            g, width = g0 + k, widths[k % n]
                            act.wait_ge(s_tr, g + 1)
                            if g >= 2:
                                act.wait_ge(s_pv, g - 1)
                            nc.scalar.copy(probsT[:, g % 2, 0:width], TB[g % 2][:, 0:width]).then_inc(s_pt, 1)

                        def copy_zT(h):
                            act.wait_ge(s_pv, g0 + (h + 1) * n)
                            if n0 + h >= 2:
                                act.wait_ge(s_y, n0 + h - 1)
                            nc.scalar.copy(zT[:, h % 2, :], VB[h % 2][0:D + 1, 0:P]).then_inc(s_zTs, 1)

                        def new_keys(k):
                            if att == 2 and k < total and k % (2 * n) == 0:
                                copy_pair(t, k // (2 * n), g0 + k)

                        for k in range(min(4, total)):
                            new_keys(k)
                        for k in range(total + 2):
                            if k < total:
                                h, c, g = k // n, k % n, g0 + k
                                if c == 0:
                                    act.wait_ge(s_max, n0 + h + 1)
                                if g >= 4:
                                    act.wait_ge(s_tr, g - 3)
                                nc.scalar.activation(probs[:, g % 4, 0:widths[c]], SB[g % 4][:, 0:widths[c]], ACT.Exp,
                                                     bias=nmax[:, h:h + 1]).then_inc(s_exp, 1)
                            new_keys(k + 4)
                            if 1 <= k <= total:
                                copy_probsT(k - 1)
                            if k >= 2 and (k - 1) % n == 0:
                                copy_zT((k - 1) // n - 1)

                    def copy_pair(t, c, g):
                        act.wait_ge(s_comb, t * H + 2 * c + 2)
                        hs = slice(2 * c, 2 * c + 2)
                        nc.scalar.copy(k_rows[:, c * P:(c + 1) * P].rearrange("p (h f) -> p h f", f=D),
                                       kv[:, hs, 0:D]).then_inc(s_ks, 1)
                        nc.scalar.copy(v2[:, t, hs, 0:D], kv[:, hs, D:2 * D]).then_inc(s_vs, 1)
                        act.wait_ge(s_kT, t * PAIRS + c + 1)
                        nc.scalar.copy(k2T[:, c, t * P:(t + 1) * P], SB[g % 4][:, 0:P]).then_inc(s_kTs, 1)

                    def embed(g):
                        act.wait_ge(s_angle, g + 1)
                        nc.scalar.activation(trig[:, 2:4, :, :], trig[:, 2:4, :, :], ACT.Sin).then_inc(s_trig, 1)

                    def front(t):
                        done = t + 1
                        act.wait_ge(s_fT, done)
                        nc.scalar.copy(fT[0:D, :], VB[0][0:D, 0:P]).then_inc(s_fTs, 1)
                        act.wait_ge(s_base, done)
                        if t:
                            act.wait_ge(s_mask, t * RG)
                        nc.scalar.activation(base2[:], VB[1][:, 0:P], ACT.Identity, bias=projb[:, 0:1])
                        nc.scalar.activation(rule_row[:], VB[1][:, P:2 * P], ACT.Identity, bias=half[:, 0:1]).then_inc(s_bases, 1)
                        act.wait_ge(s_ruled, done * RG)
                        nc.scalar.copy(hT[:], VB[0][0:D, 0:P]).then_inc(s_hTs, 1)
                        act.wait_ge(s_xT, done)
                        nc.scalar.copy(x1T[:, t * P:(t + 1) * P], VB[0][:, 0:P]).then_inc(s_xTs, 1)
                        act.wait_ge(s_q1, done)
                        for r in range(2):
                            rows = slice(r * D, (r + 1) * D)
                            last = nc.scalar.copy(q1[rows, r:H:2, :], VB[1][rows, :].rearrange("p (c q) -> p c q", q=P))
                        last.then_inc(s_q1s, 1)
                        attention(1, t)
                        act.wait_ge(s_x2T, done)
                        nc.scalar.copy(x2T[:], VB[0][:, 0:P]).then_inc(s_x2Ts, 1)
                        act.wait_ge(s_sim, done)
                        if t:
                            act.wait_ge(s_row, t)
                        for n in range(2):
                            last = nc.scalar.copy(work[:, n * BANK:(n + 1) * BANK], SB[n][:, :])
                        last.then_inc(s_sims, 1)
                        act.wait_ge(s_q2, done)
                        nc.scalar.mul(qT2[:, t % RING, :, :], VB[1][:, :].rearrange("p (c q) -> p c q", q=P),
                                      float(D) ** -0.5).then_inc(s_q2s, 1)
                        act.wait_ge(s_fd, done)
                        w = weight[:, t % RING, :, :]
                        nc.scalar.activation(w, w, ACT.Exp).then_inc(s_fe, 1)

                    def back(t):
                        act.wait_ge(s_q2s, t + 1)
                        for r in range(2):
                            rows = slice(r * D, (r + 1) * D)
                            last = nc.scalar.copy(q2[rows, r:H:2, :], qT2[rows, t % RING, :, :])
                        last.then_inc(s_q2p, 1)
                        attention(2, t)

                    for what, t in plan:
                        if what == "embed":
                            embed(t)
                        elif what == "front":
                            front(t)
                        elif what == "back":
                            back(t)

                @block.tensor
                def _(pe):
                    def attention(att, t):
                        g0, n0, n = first_chunk[att, t], first_head[att, t], n_chunks(t)
                        blocks = [min(BLK, t + 1 - BLK * c) for c in range(n)]
                        total = H * n

                        def scores(k):
                            h, c, g = k // n, k % n, g0 + k
                            if g >= 4:
                                pe.wait_ge(s_exp, g - 3)
                            if att == 2 and k % (2 * n) == 0:
                                pair = h // 2
                                pe.wait_ge(s_ks, t * PAIRS + pair + 1)
                                nc.tensor.transpose(SB[g % 4][:, 0:P], k_rows[:, pair * P:(pair + 1) * P],
                                                    ident[:]).then_inc(s_kT, 1)
                                pe.wait_ge(s_vs, t * PAIRS + pair + 1)
                                pe.wait_ge(s_kTs, t * PAIRS + pair + 1)
                            keys = slice(c * BANK, c * BANK + blocks[c] * P)
                            q = (q1 if att == 1 else q2)[:, h, :]
                            k_all = x1T[:, keys] if att == 1 else k2T[:, h // 2, keys]
                            diagonal = c == n - 1
                            last = nc.tensor.matmul(SB[g % 4][:, 0:blocks[c] * P], q, k_all, start=True, stop=not diagonal)
                            if diagonal:
                                last = nc.tensor.matmul(SB[g % 4][:, (blocks[c] - 1) * P:blocks[c] * P], ident_bf[:],
                                                        mask[:], start=False, stop=True)
                            last.then_inc(s_qk, 1)

                        def transposes(k):
                            g = g0 + k
                            pe.wait_ge(s_exp, g + 1)
                            if g >= 2:
                                pe.wait_ge(s_pt, g - 1)
                            for j in range(blocks[k % n]):
                                last = nc.tensor.transpose(TB[g % 2][:, j * P:(j + 1) * P],
                                                           probs[:, g % 4, j * P:(j + 1) * P], ident[:])
                            last.then_inc(s_tr, 1)

                        def weigh_values(k):
                            h, c, g = k // n, k % n, g0 + k
                            pe.wait_ge(s_pt, g + 1)
                            if c == 0 and n0 + h >= 2:
                                pe.wait_ge(s_acc, n0 + h - 1)
                            for j in range(blocks[c]):
                                at = c * BLK + j
                                v = x1[:, at, :] if att == 1 else v2[:, at, h, :]
                                last = nc.tensor.matmul(VB[h % 2][0:D + 1, 0:P], v, probsT[:, g % 2, j * P:(j + 1) * P],
                                                        start=at == 0, stop=at == t)
                            last.then_inc(s_pv, 1)

                        def project(h):
                            pe.wait_ge(s_zTs, n0 + h + 1)
                            nc.tensor.matmul(VB[h % 2][:, 0:D + 1], zT[:, h % 2, :], (WX1 if att == 1 else WX2)[:, h, :],
                                             start=True, stop=True).then_inc(s_y, 1)

                        for k in range(min(4, total)):
                            scores(k)
                        for k in range(total + 2):
                            if k < total:
                                transposes(k)
                            if k + 4 < total:
                                scores(k + 4)
                            if 1 <= k <= total:
                                weigh_values(k - 1)
                            if k >= 2 and (k - 1) % n == 0:
                                project((k - 1) // n - 1)
                        pe.wait_ge(s_h, order.index((att, t)) + 1)

                    def front(t):
                        done = t + 1
                        if t % GT == 0:
                            pe.wait_ge(s_four, t // GT + 1)
                        nc.tensor.transpose(VB[0][0:D, 0:P], e_a[:, t // GT % 2, t % GT, :], ident[:]).then_inc(s_fT, 1)
                        pe.wait_ge(s_fTs, done)
                        nc.tensor.matmul(VB[1][:, 0:P], projT[:], fT[:], start=True, stop=True)
                        nc.tensor.matmul(VB[1][:, P:2 * P], rule_of[:, t:t + 1].to_broadcast([P, P]), ident[:],
                                         start=True, stop=True).then_inc(s_base, 1)
                        for g in range(RG):
                            pe.wait_ge(s_mask, t * RG + g + 1)
                            for j in range(MG):
                                c = g * MG + j
                                last = nc.tensor.matmul(VB[0][0:D, 0:P], rules[:, c, :], masked[:, g % 2, j, :],
                                                        start=c == 0, stop=c == RC - 1)
                            last.then_inc(s_ruled, 1)
                        pe.wait_ge(s_hTs, done)
                        nc.tensor.transpose(VB[1][:, 0:D], hT[:], ident[0:D, 0:D]).then_inc(s_h0, 1)
                        pe.wait_ge(s_xd, done)
                        nc.tensor.transpose(VB[0][:, 0:P], xd[:].rearrange("p r f -> p (r f)"), ident[:]).then_inc(s_xT, 1)
                        pe.wait_ge(s_xTs, done)
                        for c in range(PAIRS):
                            last = nc.tensor.matmul(VB[1][:, c * P:(c + 1) * P], M1[:, c * P:(c + 1) * P],
                                                    x1T[:, t * P:(t + 1) * P], start=True, stop=True)
                        last.then_inc(s_q1, 1)
                        pe.wait_ge(s_q1s, done)
                        attention(1, t)
                        pe.wait_ge(s_x2, done)
                        nc.tensor.transpose(VB[0][:, 0:P], xd[:].rearrange("p r f -> p (r f)"), ident[:]).then_inc(s_x2T, 1)
                        pe.wait_ge(s_x2Ts, done)
                        for n in range(2):
                            last = nc.tensor.matmul(SB[n][:, :], x2T[:], A[:, n * BANK:(n + 1) * BANK], start=True, stop=True)
                        last.then_inc(s_sim, 1)
                        for c in range(PAIRS):
                            last = nc.tensor.matmul(VB[1][:, c * P:(c + 1) * P], Wq[:, c * P:(c + 1) * P], x2T[:],
                                                    start=True, stop=True)
                        last.then_inc(s_q2, 1)
                        pe.wait_ge(s_sims, done)
                        pe.wait_ge(s_q2s, done)

                    def back(t):
                        pe.wait_ge(s_q2p, t + 1)
                        attention(2, t)

                    for what, t in plan:
                        if what == "front":
                            front(t)
                        elif what == "back":
                            back(t)

                @block.vector
                def _(dve):
                    steps = [0]

                    def link(ins):
                        steps[0] += 1
                        ins.then_inc(s_dve, 1)
                        dve.wait_ge(s_dve, steps[0])

                    V = nc.vector

                    def divide_ids():
                        f, qa, qb, r = (work[:, n * T:(n + 1) * T] for n in range(4))
                        r0 = quotient[:]
                        inv = float(np.float32(1.0) / np.float32(VOCAB))
                        hi, lo = float(VOCAB // 256 * 256), float(VOCAB % 256)
                        dve.wait_ge(s_ids, 16)
                        link(V.tensor_copy(f, ids[:]))
                        link(V.tensor_scalar(r0, f, inv, None, ALU.mult))
                        link(V.tensor_scalar(qa.bitcast(I32), r0.bitcast(I32), -4096, None, ALU.bitwise_and))
                        link(V.tensor_tensor(qb, r0, qa, ALU.subtract))
                        link(V.scalar_tensor_tensor(r, qa, -hi, f, ALU.mult, ALU.add))
                        link(V.scalar_tensor_tensor(r, qa, -lo, r, ALU.mult, ALU.add))
                        link(V.scalar_tensor_tensor(r, qb, -hi, r, ALU.mult, ALU.add))
                        link(V.scalar_tensor_tensor(r, qb, -lo, r, ALU.mult, ALU.add))
                        link(V.scalar_tensor_tensor(r0, r, inv, r0, ALU.mult, ALU.add))
                        link(V.tensor_scalar(angular[:], freq[:], float(np.float32(2.0 * math.pi)), None, ALU.mult))

                    def embed(g):
                        shape = [P, GT, D]
                        ang, k, sn, cs = (trig[:, n, :, :] for n in range(4))
                        link(V.tensor_tensor(ang, angular[:].unsqueeze(1).to_broadcast(shape),
                                             quotient[:, g * GT:(g + 1) * GT].unsqueeze(2).to_broadcast(shape), ALU.mult))
                        link(V.tensor_scalar(k, ang, 1.0 / (2.0 * math.pi), ROUND, ALU.mult, ALU.add))
                        link(V.tensor_scalar(k, k, ROUND, None, ALU.subtract))
                        for c in two_pi_parts():
                            link(V.scalar_tensor_tensor(ang, k, -c, ang, ALU.mult, ALU.add))
                        link(V.tensor_scalar(sn, ang, 3.1415925, -3.1415925, ALU.min, ALU.max))
                        link(V.scalar_tensor_tensor(cs, sn, -1.0, sn, ALU.mult, ALU.max))
                        V.tensor_scalar(cs, cs, -1.0, math.pi / 2, ALU.mult, ALU.add).then_inc(s_angle, 1)
                        dve.wait_ge(s_trig, g + 1)
                        dve.wait_ge(s_emb[g % 2], 16 * 3 * GT * (g // 2 + 1))
                        a, bb = e_a[:, g % 2, :, :], e_b[:, g % 2, :, :]
                        V.tensor_tensor(a, a, cs, ALU.mult)
                        link(V.tensor_tensor(bb, bb, sn, ALU.mult))
                        V.tensor_copy(rule_of[:, g * GT:(g + 1) * GT], rule_i[:, g % 2, :])
                        V.tensor_tensor(a, a, bb, ALU.add).then_inc(s_four, 1)

                    def layernorm_scale(src):
                        v, y, u = rs[:, 0:1], rs[:, 1:2], rs[:, 2:3]
                        link(V.bn_stats(stats[:], src))
                        link(V.bn_aggr(meanvar[:], stats[:]))
                        link(V.tensor_scalar(v, meanvar[:, 1:2], EPS, None, ALU.add))
                        link(V.tensor_scalar(u.bitcast(I32), v.bitcast(I32), 1, None, ALU.logical_shift_right))
                        link(V.tensor_scalar(y.bitcast(I32), u.bitcast(I32), -1.0, float(RSQRT_SEED), ALU.mult, ALU.add))
                        for _ in range(3):
                            link(V.tensor_scalar(u, y, y, v, ALU.mult, ALU.mult))
                            link(V.tensor_scalar(u, u, -0.5, 1.5, ALU.mult, ALU.add))
                            link(V.tensor_tensor(y, y, u, ALU.mult))

                    def combine_at(stage, tile, place):
                        for t, h in heads_at.get((stage, tile, place), ()):
                            n = t * H + h
                            slot = n % SLOTS
                            uses = len(range(slot, T * H, SLOTS))
                            if t:
                                dve.wait_ge(s_ks, (t - 1) * PAIRS + h // 2 + 1)
                                dve.wait_ge(s_vs, (t - 1) * PAIRS + h // 2 + 1)
                            dve.wait_ge(s_g[slot], 256 * (n // SLOTS + 1))
                            w = weight[:, t % RING, h, :]
                            acc = kv[:, h, :]
                            for r in range(TOPK):
                                if r == 0:
                                    last = V.tensor_scalar(acc, G[:, slot, 0, :], w[:, 0:1], None, ALU.mult)
                                else:
                                    link(last)
                                    last = V.scalar_tensor_tensor(acc, G[:, slot, r, :], w[:, r:r + 1], acc, ALU.mult, ALU.add)
                            last.then_inc(s_comb, 1)

                    def attention(att, t):
                        g0, n0, n = first_chunk[att, t], first_head[att, t], n_chunks(t)
                        widths = [min(BLK, t + 1 - BLK * c) * P for c in range(n)]
                        before, total = (h0[:], h1[:, t % RING, :]) if att == 1 else (h1[:, t % RING, :], obuf[:, t % 2, :])

                        def add(h):
                            dve.wait_ge(s_y, n0 + h + 1)
                            y = VB[h % 2]
                            link(V.reciprocal(rec[:, h % 2:h % 2 + 1], y[:, D:D + 1]))
                            last = V.scalar_tensor_tensor(total, y[:, 0:D], rec[:, h % 2:h % 2 + 1],
                                                          total if h else before, ALU.mult, ALU.add)
                            last.then_inc(s_acc, 1)
                            dve.wait_ge(s_acc, n0 + h + 1)

                        for h in range(H + 2):
                            if h < H:
                                combine_at("front" if att == 1 else "back", t, h)
                                for c in range(n):
                                    g = g0 + h * n + c
                                    dve.wait_ge(s_qk, g + 1)
                                    dst = nmax[:, h:h + 1] if n == 1 else mx[:, h % 2, c:c + 1]
                                    last = V.tensor_reduce(dst, SB[g % 4][:, 0:widths[c]], AX, ALU.max, negate=n == 1)
                                if n > 1:
                                    link(last)
                                    last = V.tensor_reduce(nmax[:, h:h + 1], mx[:, h % 2, 0:n], AX, ALU.max, negate=True)
                                last.then_inc(s_max, 1)
                            if h >= 2:
                                add(h - 2)
                        nc.vector.sem_inc(s_h, 1)

                    def top16(values, first, second, index, n):
                        for rank, place_ in ((slice(0, 8), 0), (slice(8, 16), 1)):
                            for j in range(n):
                                last = V.max(first[:, j, rank], values[:, j, :])
                            link(last)
                            for j in range(n):
                                last = V.max_index(index[:, j, rank], first[:, j, rank], values[:, j, :])
                            if place_ == 0:
                                for j in range(n):
                                    last = V.match_replace(values[:, j, :], first[:, j, rank], values[:, j, :], LOWEST)
                            link(last)

                    def front(t):
                        done = t + 1
                        dve.wait_ge(s_bases, done)
                        for g in range(RG):
                            n = t * RG + g
                            if t * RG + g >= 2:
                                dve.wait_ge(s_ruled, n - 1)
                            for j in range(MG):
                                last = V.scalar_tensor_tensor(masked[:, g % 2, j, :], rule_row[:], 2.0 * (g * MG + j),
                                                              base2[:], ALU.is_equal, ALU.mult)
                            last.then_inc(s_mask, 1)
                        dve.wait_ge(s_h0, done)
                        link(V.tensor_copy(h0[:], VB[1][:, 0:D]))
                        layernorm_scale(h0[:])
                        V.tensor_scalar(xd[:], h0[:].unsqueeze(1).to_broadcast([P, 2, D]), meanvar[:, 0:1], rs[:, 1:2],
                                        ALU.subtract, ALU.mult)
                        V.tensor_scalar(x1[:, t, 0:D], h0[:], meanvar[:, 0:1], rs[:, 1:2],
                                        ALU.subtract, ALU.mult).then_inc(s_xd, 1)
                        combine_at("front", t, "normed")
                        attention(1, t)
                        h = h1[:, t % RING, :]
                        layernorm_scale(h)
                        V.tensor_scalar(xd[:], h.unsqueeze(1).to_broadcast([P, 2, D]), meanvar[:, 0:1], rs[:, 1:2],
                                        ALU.subtract, ALU.mult).then_inc(s_x2, 1)
                        combine_at("front", t, "added")

                        dve.wait_ge(s_sims, done)
                        top16(scores_pk, sv, None, si, NP)
                        combine_at("front", t, "parts")
                        s0, s1, i0, i1 = sv[:, 0:H, :], sv[:, H:NP, :], si[:, 0:H, :], si[:, H:NP, :]
                        link(V.scalar_tensor_tensor(jrow[:], i1, float(NKEYS), head_row[:], ALU.mult, ALU.add))
                        for a, rows, n, at in RUNS:
                            for dst, left, right in ((cand, s0, s1), (cand_row, i0, jrow)):
                                if rows == 1:
                                    o, l, r = (dst[:, :, at:at + n], left[:, :, a:a + 1].to_broadcast([P, H, n]),
                                               right[:, :, 0:n])
                                else:
                                    shape = [P, H, rows, n]
                                    o = dst[:, :, at:at + rows * n].rearrange("p h (a b) -> p h a b", b=n)
                                    l = left[:, :, a:a + rows].unsqueeze(3).to_broadcast(shape)
                                    r = right[:, :, 0:n].unsqueeze(2).to_broadcast(shape)
                                last = V.tensor_tensor(o, l, r, ALU.add)
                        link(last)
                        link(V.tensor_tensor(cand_row[:], cand_row[:], place[:].unsqueeze(1).to_broadcast([P, H, NC]), ALU.add))
                        top16(cand, fv, None, fpos, H)
                        w = weight[:, t % RING, :, :]
                        V.tensor_tensor(w, fv[:], fv[:, :, 0:1].to_broadcast([P, H, TOPK]), ALU.subtract).then_inc(s_fd, 1)
                        link(V.tensor_scalar(fcode[:], fpos[:], float(CODE), None, ALU.mult))
                        for e in range(H // EQH):
                            hs = slice(e * EQH, (e + 1) * EQH)
                            far = work[:].rearrange("p (h r c) -> p h r c", h=EQH, c=NC)
                            shape = [P, EQH, TOPK, NC]
                            link(V.tensor_tensor(far, cand_row[:, hs, :].unsqueeze(2).to_broadcast(shape),
                                                 fcode[:, hs, :].unsqueeze(3).to_broadcast(shape), ALU.subtract))
                            link(V.tensor_reduce(fcode[:, hs, :], far, AX, ALU.min, apply_absolute_value=True))
                        dve.wait_ge(s_fe, done)
                        link(V.tensor_reduce(wsum[:], w, AX, ALU.add))
                        link(V.reciprocal(wsum[:], wsum[:]))
                        link(V.tensor_tensor(w, w, wsum[:].unsqueeze(2).to_broadcast([P, H, TOPK]), ALU.mult))
                        V.tensor_copy(row_u[:, t % RING, :], fcode[:].rearrange("p h r -> p (h r)")).then_inc(s_row, 1)
                        combine_at("front", t, "rows")

                    def back(t):
                        if t >= 2:
                            dve.wait_ge(s_out[t % 2], 16 * (t // 2))
                        attention(2, t)

                    divide_ids()
                    for what, t in plan:
                        if what == "embed":
                            embed(t)
                        elif what == "front":
                            front(t)
                        elif what == "back":
                            back(t)

        with nc.Fori(0, NB) as b:
            batch(b)
            nc.all_engine_barrier(sems_to_clear=batch_sems)


_INS = ["x", "L0_tok_a_n", "L0_tok_b_n", "L0_tok_rule_transform", "L0_tok_token_rules", "L0_tok_proj_w",
        "L0_tok_proj_b", "L0_attn_key_matrices", "L0_attn_query_matrices", "L0_attn_value_in_matrices",
        "L0_attn_value_out_matrices", "L0_ffn_Wq_pk", "L0_ffn_pk_keys", "L0_ffn_Wq", "L0_ffn_keys_table",
        "L0_ffn_values_table", "L0_ffn_Wo"]


def kernel(**inputs):
    import numpy as _np
    import concourse.bacc as _bacc
    from concourse import mybir as _mybir
    from concourse.bass_utils import run_bass_kernel_spmd as _run

    nc = _bacc.Bacc("TRN2", target_bir_lowering=False, num_devices=1)
    arrays, args = {}, []
    for name in _INS:
        a = _np.ascontiguousarray(inputs[name])
        arrays[f"in_{name}"] = a
        args.append(nc.dram_tensor(f"in_{name}", a.shape, _mybir.dt.from_np(a.dtype), kind="ExternalInput").ap())
    b, s = inputs["x"].shape
    out = nc.dram_tensor("out_rows", (b, s, inputs["L0_tok_a_n"].shape[1]), _mybir.dt.float32, kind="ExternalOutput").ap()
    lm_block(nc, *args, out)
    r = _run(nc, [arrays], core_ids=[0])
    return r.results[0]["out_rows"]
```

```python
import math
from contextlib import ExitStack

import numpy as np

import concourse.bass as bass
from concourse import mybir

F32 = mybir.dt.float32
BF16 = mybir.dt.bfloat16
I32 = mybir.dt.int32
U32 = mybir.dt.uint32
ALU = mybir.AluOpType
ACT = mybir.ActivationFunctionType
AX = mybir.AxisListType.X

P = 128
BANK = 512
BLK = BANK // P
EPS = 1e-5
LOWEST = -3.0e38
TOPK = 16
RSQRT_SEED = 0x5F3759DF
ROUND = 1.5 * 2.0**23


def two_pi_parts():
    c1 = np.float32(6.28125)
    c2 = np.float32(np.floor((2 * math.pi - float(c1)) * 2.0**26) / 2.0**26)
    c3 = np.float32(2 * math.pi - float(c1) - float(c2))
    return float(c1), float(c2), float(c3)


def staircase():
    runs, at = [], 0
    for a in range(TOPK):
        n = TOPK // (a + 1)
        if runs and runs[-1][2] == n:
            runs[-1][1] += 1
        else:
            runs.append([a, 1, n, at])
        at += n
    return runs, at


def lm_block(nc, x, a_n, b_n, rule_transform, token_rules, proj_w, proj_b, key_m, query_m, vin_m,
             vout_m, wq_pk, pk_keys, wq, keys_table, values_table, wo, out):
    NB, S = x.shape
    T = S // P
    VOCAB, D = a_n.shape
    H = key_m.shape[0]
    PAIRS = H // 2
    NRULES = rule_transform.shape[0]
    RC = NRULES // 2
    MG = 5
    RG = RC // MG
    NKEYS = pk_keys.shape[1]
    ROWS = keys_table.shape[0]
    HROWS = ROWS // H
    NP = 2 * H
    RUNS, NC = staircase()
    SLOTS = 5
    EQH = 2
    LEAD = 2
    RING = LEAD + 1
    GT = 4
    CODE = 2 * ROWS
    assert CODE * NC < 2**24
    RS = RG // 5
    assert LEAD == 2 and T > 2 * LEAD
    assert H == 8 and RG == 5 * RS and H // EQH == 4
    assert D == 64 and NKEYS == D and NRULES % (2 * MG) == 0

    kv_table = nc.dram_tensor("kv_table", [ROWS, 2 * D], F32, kind="Internal").ap()

    plan = [("embed", 0), ("rows", 0)]
    rows_beside = lambda t: 0 < t and t + 1 < T

    def plan_front(t):
        if t < T:
            if (t + 1) % GT == 0 and t + 1 < T:
                plan.append(("embed", (t + 1) // GT))
            plan.append(("front", t))

    for t in range(LEAD):
        plan_front(t)
        plan.append(("queries", t))
        plan.append(("choice", t))
        if t == 0:
            plan.append(("rows", 1))
    for t in range(T):
        if t:
            plan.append(("back", t - 1))
        plan_front(t + LEAD)
    plan.append(("back", T - 1))

    queries_beside = lambda att, t, head: att == 2 and t + LEAD < T and head < 5

    def choice_beside(att, t, head):
        if att == 2 and t + LEAD < T and 4 <= head < H:
            return t + LEAD, range(3, 8) if t + LEAD == T - 1 and head == 7 else (head - 4,)
        if att == 1 and t > LEAD and head < H and head % 2 == 0:
            return t - 1, (4 + head // 2,)
        return None, ()

    heads_at = {}
    for t in range(T):
        if t == 0:
            places = [("front", 1, h) for h in (3, 5, 7)] + [("front", 2, h) for h in (0, 1, 3, 5, 7)]
        elif t + LEAD < T:
            places = ([("back", t - 1, h) for h in (1, 2, 3, 7)] +
                      [("front", t + LEAD, h) for h in (1, 3, 5, 7)])
        else:
            first = 4 if t == T - 1 else 0
            places = [("back", t - 1, first + h) for h in range(4)] + [("back", t, h) for h in range(4)]
        for h in range(H):
            heads_at.setdefault(places[h], []).append((t, h))

    order = [(1 if what == "front" else 2, t) for what, t in plan if what in ("front", "back")]
    n_chunks = lambda t: (t + BLK) // BLK
    first_chunk, first_head, CHUNKS = {}, {}, 0
    for n, at in enumerate(order):
        first_chunk[at], first_head[at] = CHUNKS, n * H
        CHUNKS += H * n_chunks(at[1])

    with ExitStack() as ctx:
        def sb(name, shape, dt=F32):
            return ctx.enter_context(nc.sbuf_tensor(name, shape, dt))

        def sem(name):
            return ctx.enter_context(nc.semaphore(name))

        k2T = sb("k2T", [P, PAIRS, S])
        v2 = sb("v2", [P, T, H, D + 1])
        x1T = sb("x1T", [P, S])
        x1 = sb("x1", [P, T, D + 1])
        e_a = sb("e_a", [P, 2, GT, D])
        e_b = sb("e_b", [P, 2, GT, D])
        quotient = sb("quotient", [P, T])
        rule_of = sb("rule_of", [P, T])
        ids = sb("ids", [P, T], I32)
        rule_i = sb("rule_i", [P, 2, GT], I32)
        rules = sb("rules", [P, RC, D])
        M1 = sb("M1", [P, H * D])
        WX1 = sb("WX1", [D + 1, H, D + 1])
        WX2 = sb("WX2", [D + 1, H, D + 1])
        A = sb("A", [P, NP * NKEYS])
        Wq = sb("Wq", [P, H * D])
        projT = sb("projT", [P, 2 * D])
        projb = sb("projb", [P, 1])
        ident = sb("ident", [P, P])
        ident_bf = sb("ident_bf", [P, P], BF16)
        mask = sb("mask", [P, P], BF16)
        half = sb("half", [P, 1])
        head_row = sb("head_row", [P, H, TOPK])
        place = sb("place", [P, NC])
        freq = sb("freq", [P, D])
        angular = sb("angular", [P, D])
        fT = sb("fT", [P, P])
        base2 = sb("base2", [P, P])
        rule_row = sb("rule_row", [P, P])
        masked = sb("masked", [P, 2, MG, P])
        h0 = sb("h0", [P, D])
        hT = sb("hT", [D, P])
        h1 = sb("h1", [P, RING, D])
        stats = sb("stats", [P, 6])
        meanvar = sb("meanvar", [P, 2])
        rs = sb("rs", [P, 4])
        xd = sb("xd", [P, 2, D])
        x2T = sb("x2T", [P, P])
        qT2 = sb("qT2", [P, RING, PAIRS, P])
        q1 = sb("q1", [P, H, P])
        q2 = sb("q2", [P, H, P])
        work = sb("work", [P, EQH * TOPK * NC])
        sv = sb("sv", [P, NP, TOPK])
        si = sb("si", [P, NP, TOPK], U32)
        jrow = sb("jrow", [P, H, TOPK])
        cand = sb("cand", [P, H, NC])
        cand_row = sb("cand_row", [P, H, NC])
        fv = sb("fv", [P, H, TOPK])
        fpos = sb("fpos", [P, H, TOPK], U32)
        fcode = sb("fcode", [P, H, TOPK])
        wsum = sb("wsum", [P, H])
        weight = sb("weight", [P, RING, H, TOPK])
        row_u = sb("row_u", [P, RING, H * TOPK], U32)
        G = sb("G", [P, SLOTS, TOPK, 2 * D])
        kv = sb("kv", [P, H, 2 * D])
        k_rows = sb("k_rows", [P, H * D])
        probs = sb("probs", [P, 4, BANK])
        probsT = sb("probsT", [P, 2, BANK])
        mx = sb("mx", [P, 2, 4])
        nmax = sb("nmax", [P, H])
        rec = sb("rec", [P, 2])
        zT = sb("zT", [D + 1, 2, P])
        obuf = sb("obuf", [P, 2, D])

        bank = [ctx.enter_context(nc.psum_tensor(f"bank{i}", [P, BANK], F32)) for i in range(8)]
        SB, TB, VB, FB = bank[0:4], bank[4], bank[5:7], bank[7]

        trig = masked[:].rearrange("p a b c -> p (a b c)")[:, 0:4 * GT * D].rearrange("p (n t f) -> p n t f", n=4, f=D)
        scores_pk = work[:, 0:NP * NKEYS].rearrange("p (n k) -> p n k", k=NKEYS)
        raw = lambda n, width: k2T[0:D, n // 4, (n % 4) * 512:(n % 4) * 512 + width]
        rawK, rawQ, rawVin, rawVout, rawWpk, rawPk, rawProj = (raw(n, 512) for n in range(7))
        KT, QT, VinT = (k2T[0:D, 2, n * 512:(n + 1) * 512] for n in range(3))
        WpkT = k2T[:, 2, 1536:1536 + 256].rearrange("p (c e) -> p c e", e=D)
        pkD = k2T[:, 3, 0:1024].rearrange("p (c k) -> p c k", c=4)

        s_wload = sem("weights_loaded"); s_table = sem("table_merged"); s_rules = sem("rules_loaded")
        s_const = sem("constants_made"); s_zero = sem("zeros_made"); s_cleared = sem("cleared"); s_pool = sem("pool_step")
        s_wT = sem("weights_transposed"); s_wTs = sem("weights_transposed_in_sbuf")
        s_wP = sem("weight_products"); s_wPs = sem("weight_products_in_sbuf")
        s_ids = sem("ids_loaded"); s_emb = [sem(f"embedding_gathered{n}") for n in range(2)]
        s_dve = sem("vector_step")
        s_angle = sem("angles"); s_trig = sem("sin_cos"); s_four = sem("fourier_ready")
        s_fT = sem("fourier_transposed"); s_fTs = sem("fourier_transposed_in_sbuf")
        s_base = sem("base_and_rule"); s_bases = sem("base_and_rule_in_sbuf")
        s_mask = sem("masked_ready"); s_ruled = sem("masked_used");
        s_xd = sem("x1_ready"); s_xT = sem("x1_transposed"); s_xTs = sem("x1T_in_sbuf")
        s_q1 = sem("q1"); s_q1s = sem("q1_in_sbuf")
        s_qk = sem("scores_ready"); s_max = sem("max_ready"); s_exp = sem("probs_ready")
        s_tr = sem("probs_transposed"); s_pt = sem("probsT_in_sbuf"); s_pv = sem("pv_done")
        s_zTs = sem("zT_in_sbuf"); s_y = sem("head_projected"); s_acc = sem("head_added")
        s_hTs = sem("hT_in_sbuf"); s_h0 = sem("h0_ready")
        s_q2p = sem("q2_padded")
        s_h = sem("residual_added")
        s_x2 = sem("x2_ready"); s_x2T = sem("x2_transposed"); s_x2Ts = sem("x2T_in_sbuf")
        s_sim = sem("pk_scores"); s_sims = sem("pk_scores_in_sbuf")
        s_q2 = sem("q2"); s_q2s = sem("q2_in_sbuf")
        s_fd = sem("final_less_max"); s_fe = sem("final_exp")
        s_row = sem("rows_chosen")
        s_g = [sem(f"gathered{n}") for n in range(SLOTS)]
        s_comb = sem("head_combined")
        s_ks = sem("k_rows_copied"); s_kT = sem("k_transposed"); s_kTs = sem("kT_in_sbuf"); s_vs = sem("v_in_sbuf")
        s_out = [sem(f"stored{n}") for n in range(2)]


        batch_sems = range(s_ids.num, s_out[-1].num + 1)

        with nc.Block() as setup:

            @setup.sync
            def _(sp):
                def load(dst, src):
                    sp.dma_start(dst, src).then_inc(s_wload, 16)

                load(rawK.rearrange("e (n d) -> e n d", d=D), key_m.rearrange("n e d -> e n d"))
                load(rawQ.rearrange("e (n d) -> e n d", d=D), query_m.rearrange("n e d -> e n d"))
                load(rawVin.rearrange("e (n d) -> e n d", d=D), vin_m.rearrange("n p d -> p n d"))
                load(rawVout.rearrange("e (n d) -> e n d", d=D), vout_m.rearrange("n d e -> d n e"))
                load(rawWpk, wq_pk)
                load(rawPk.rearrange("k (p c) -> k p c", p=2), pk_keys.rearrange("p k h d -> k p (h d)"))
                load(rawProj[:, 0:D], proj_w)
                load(Wq[0:D, :], wq)
                sp.wait_ge(s_zero, 1)
                load(WX2[0:D, :, 0:D], wo.rearrange("(h d) e -> d h e", h=H))
                for r in range(2):
                    load(projb[r * D:(r + 1) * D, :], proj_b.unsqueeze(1))
                for r in range(2):
                    sp.dma_start(rules[r * D:(r + 1) * D, :, :],
                                 rule_transform.rearrange("(c r) d e -> r d c e", r=2)[r]).then_inc(s_rules, 16)


            @setup.gpsimd
            def _(pool):
                steps = [0]

                def step(ins):
                    steps[0] += 1
                    ins.then_inc(s_pool, 1)
                    pool.wait_ge(s_pool, steps[0])

                step(nc.gpsimd.memset(ident[:], 0.0))
                step(nc.gpsimd.affine_select(out=ident[:], in_=ident[:], compare_op=ALU.not_equal, fill=1.0,
                                             base=0, pattern=[[-1, P]], channel_multiplier=1))
                step(nc.gpsimd.tensor_copy(ident_bf[:], ident[:]))
                step(nc.gpsimd.memset(mask[:], 0.0))
                step(nc.gpsimd.affine_select(out=mask[:], in_=mask[:], compare_op=ALU.is_ge, fill=LOWEST,
                                             base=0, pattern=[[-1, P]], channel_multiplier=1))
                step(nc.gpsimd.memset(half[0:D, :], 0.0))
                nc.gpsimd.iota(head_row[:], pattern=[[HROWS, H], [0, TOPK]], base=0, channel_multiplier=0,
                               allow_small_or_imprecise_dtypes=True)
                nc.gpsimd.iota(place[:], pattern=[[1, NC]], base=0, channel_multiplier=0,
                               allow_small_or_imprecise_dtypes=True)
                step(nc.gpsimd.iota(freq[:], pattern=[[1, D]], base=1, channel_multiplier=0,
                               allow_small_or_imprecise_dtypes=True))
                step(nc.gpsimd.tensor_scalar(place[:], place[:], float(CODE), None, ALU.mult))
                nc.gpsimd.memset(half[D:P, :], -1.0).then_inc(s_const, 1)


            @setup.scalar
            def _(act):
                act.wait_ge(s_wload, 16 * 11)
                act.wait_ge(s_rules, 32)
                act.dma_start(kv_table[:, 0:D], keys_table).then_inc(s_table, 16)
                act.dma_start(kv_table[:, D:2 * D], values_table).then_inc(s_table, 16)

                act.wait_ge(s_wT, 1)
                act.wait_ge(s_zero, 1)
                for dst, src in ((KT, SB[0]), (QT, SB[1]), (VinT, SB[2])):
                    nc.scalar.copy(dst, src[0:D, :])
                nc.scalar.copy(WpkT, SB[3][:, 0:256].rearrange("p (c e) -> p c e", e=D))
                for c in range(4):
                    for r in range(4):
                        nc.scalar.copy(pkD[32 * r:32 * r + 32, c, D * r:D * r + D],
                                       SB[3][32 * r:32 * r + 32, 256 + D * c:256 + D * c + D])
                for r in range(2):
                    last = nc.scalar.copy(projT[0:D, r * D:(r + 1) * D], TB[0:D, 0:D])
                last.then_inc(s_wTs, 1)
                act.wait_ge(s_wP, 1)
                nc.scalar.copy(M1[0:D, :], SB[0][0:D, :])
                nc.scalar.copy(WX1[0:D, :, 0:D], SB[1][0:D, :].rearrange("p (n e) -> p n e", e=D))
                for n in range(2):
                    last = nc.scalar.copy(A[0:D, n * 512:(n + 1) * 512], SB[2 + n][0:D, :])
                last.then_inc(s_wPs, 1)


            @setup.tensor
            def _(pe):
                pe.wait_ge(s_wload, 16 * 11)
                pe.wait_ge(s_const, 1)
                i64 = ident[0:D, 0:D]
                for n in range(H):
                    c = slice(n * D, (n + 1) * D)
                    nc.tensor.transpose(SB[0][0:D, c], rawK[:, c], i64)
                    nc.tensor.transpose(SB[1][0:D, c], rawQ[:, c], i64)
                    nc.tensor.transpose(SB[2][0:D, c], rawVin[:, c], i64)
                for c in range(4):
                    nc.tensor.transpose(SB[3][:, c * D:(c + 1) * D], rawWpk[:, c * P:(c + 1) * P], i64)
                    nc.tensor.transpose(SB[3][:, 256 + c * D:256 + (c + 1) * D], rawPk[:, c * P:(c + 1) * P], i64)
                nc.tensor.transpose(TB[0:D, 0:D], rawProj[:, 0:D], i64).then_inc(s_wT, 1)
                pe.wait_ge(s_wTs, 1)
                for n in range(H):
                    c = slice(n * D, (n + 1) * D)
                    nc.tensor.matmul(SB[0][0:D, c], KT[:, c], QT[:, c], start=True, stop=True)
                    nc.tensor.matmul(SB[1][0:D, c], VinT[:, c], rawVout[:, c], start=True, stop=True)
                for c in range(4):
                    last = nc.tensor.matmul(SB[2 + c // 2][0:D, (c % 2) * 256:(c % 2 + 1) * 256], WpkT[:, c, :],
                                            pkD[:, c, :], start=True, stop=True)
                last.then_inc(s_wP, 1)
                pe.wait_ge(s_wPs, 1)
                pe.wait_ge(s_rules, 32)


            @setup.vector
            def _(dve):
                for zero in (M1[D:P, :], A[D:P, :], Wq[D:P, :], projT[D:P, :], fT[D:P, :], q1[:], q2[:], WX1[:], WX2[:]):
                    last = nc.vector.memset(zero, 0.0)
                last.then_inc(s_cleared, 1)
                dve.wait_ge(s_cleared, 1)
                nc.vector.memset(WX1[D:D + 1, :, D:D + 1], 1.0)
                nc.vector.memset(WX2[D:D + 1, :, D:D + 1], 1.0)
                nc.vector.memset(pkD, 0.0).then_inc(s_zero, 1)
                nc.vector.memset(x1[:, :, D:D + 1], 1.0)
                nc.vector.memset(v2[:, :, :, D:D + 1], 1.0)


        def batch(b):
            with nc.Block() as block:
                @block.sync
                def _(sp):
                    x_tiles = x.rearrange("b (t p) -> b p t", p=P)
                    out_tiles = out.rearrange("b (t p) e -> b t p e", p=P)
                    with nc.allow_non_contiguous_dma(reason="one id for each partition"):
                        sp.dma_start(ids[:], x_tiles[bass.ds(b, 1), :, :].rearrange("o p t -> p (o t)")).then_inc(s_ids, 16)
                    for t in range(T):
                        sp.wait_ge(s_h, order.index((2, t)) + 1)
                        sp.dma_start(out_tiles[bass.ds(b, 1), t, :, :].rearrange("o p e -> p (o e)"),
                                     obuf[:, t % 2, :]).then_inc(s_out[t % 2], 16)
                    for n in range(2):
                        sp.wait_ge(s_out[n], 16 * T // 2)

                @block.gpsimd
                def _(pool):
                    def embedding(g):
                        if g >= 2:
                            pool.wait_ge(s_fT, GT * (g - 1))
                        for j in range(GT):
                            t = g * GT + j
                            at = bass.IndirectOffsetOnAxis(ap=ids[:, t:t + 1].bitcast(U32), axis=0)
                            e = g % 2
                            pool.indirect_dma_start(e_a[:, e, j, :], None, a_n, at).then_inc(s_emb[e], 16)
                            pool.indirect_dma_start(e_b[:, e, j, :], None, b_n, at).then_inc(s_emb[e], 16)
                            pool.indirect_dma_start(rule_i[:, e, j:j + 1], None, token_rules.unsqueeze(1), at).then_inc(s_emb[e], 16)

                    pool.wait_ge(s_ids, 16)
                    embedding(0)
                    embedding(1)
                    pool.wait_ge(s_table, 32)
                    for t in range(T):
                        g = (t + LEAD + 1) // GT
                        if (t + LEAD + 1) % GT == 0 and 2 <= g < T // GT:
                            embedding(g)
                        for h in range(H):
                            pool.wait_ge(s_row, t * (H // EQH) + h // EQH + 1)
                            n = t * H + h
                            if n >= SLOTS:
                                pool.wait_ge(s_comb, n - SLOTS + 1)
                            for r in range(TOPK):
                                c = h * TOPK + r
                                pool.indirect_dma_start(
                                    G[:, n % SLOTS, r, :], None, kv_table,
                                    bass.IndirectOffsetOnAxis(ap=row_u[:, t % RING, c:c + 1], axis=0),
                                ).then_inc(s_g[n % SLOTS], 16)
                    for e in range(2):
                        pool.wait_ge(s_emb[e], 16 * 3 * T // 2)
                    for slot in range(SLOTS):
                        pool.wait_ge(s_g[slot], 16 * TOPK * len(range(slot, T * H, SLOTS)))
                    nc.gpsimd.dma_reset(batch_sems)

                @block.scalar
                def _(act):
                    def attention(att, t):
                        g0, n0, n = first_chunk[att, t], first_head[att, t], n_chunks(t)
                        widths = [min(BLK, t + 1 - BLK * c) * P for c in range(n)]
                        total = H * n

                        def copy_probsT(k):
                            g, width = g0 + k, widths[k % n]
                            act.wait_ge(s_tr, g + 1)
                            if g >= 2:
                                act.wait_ge(s_pv, g - 1)
                            nc.scalar.copy(probsT[:, g % 2, 0:width], TB[:, 0:width]).then_inc(s_pt, 1)

                        def copy_zT(h):
                            act.wait_ge(s_pv, g0 + (h + 1) * n)
                            if n0 + h >= 2:
                                act.wait_ge(s_y, n0 + h - 1)
                            nc.scalar.copy(zT[:, h % 2, :], VB[h % 2][0:D + 1, 0:P]).then_inc(s_zTs, 1)

                        def new_keys(k):
                            if att == 2 and k < total and k % (2 * n) == 0:
                                copy_pair(t, k // (2 * n), g0 + k)

                        for k in range(min(4, total)):
                            new_keys(k)
                        for k in range(total + 2):
                            if n > 1 and 1 <= k <= total:
                                copy_probsT(k - 1)
                            if k < total:
                                h, c, g = k // n, k % n, g0 + k
                                if c == 0:
                                    beside(att, t, h)
                                    act.wait_ge(s_max, n0 + h + 1)
                                if g >= 4:
                                    act.wait_ge(s_tr, g - 3)
                                nc.scalar.activation(probs[:, g % 4, 0:widths[c]], SB[g % 4][:, 0:widths[c]], ACT.Exp,
                                                     bias=nmax[:, h:h + 1]).then_inc(s_exp, 1)
                            if n == 1 and 1 <= k <= total:
                                copy_probsT(k - 1)
                            new_keys(k + 4)
                            if k >= 2 and (k - 1) % n == 0:
                                copy_zT((k - 1) // n - 1)

                    def copy_pair(t, c, g):
                        act.wait_ge(s_comb, t * H + 2 * c + 2)
                        hs = slice(2 * c, 2 * c + 2)
                        nc.scalar.copy(k_rows[:, c * P:(c + 1) * P].rearrange("p (h f) -> p h f", f=D),
                                       kv[:, hs, 0:D]).then_inc(s_ks, 1)
                        nc.scalar.copy(v2[:, t, hs, 0:D], kv[:, hs, D:2 * D]).then_inc(s_vs, 1)
                        act.wait_ge(s_kT, t * PAIRS + c + 1)
                        nc.scalar.copy(k2T[:, c, t * P:(t + 1) * P], SB[g % 4][:, 0:P]).then_inc(s_kTs, 1)

                    def embed(g):
                        act.wait_ge(s_angle, g + 1)
                        nc.scalar.activation(trig[:, 2:4, :, :], trig[:, 2:4, :, :], ACT.Sin).then_inc(s_trig, 1)

                    def row_step(t, step):
                        done = t + 1
                        if step == 0:
                            act.wait_ge(s_fT, done)
                            nc.scalar.copy(fT[0:D, :], FB[0:D, 0:P]).then_inc(s_fTs, 1)
                        elif step == 1:
                            act.wait_ge(s_base, done)
                            if t:
                                act.wait_ge(s_mask, t * RG)
                            nc.scalar.activation(base2[:], FB[:, P:2 * P], ACT.Identity, bias=projb[:, 0:1])
                            nc.scalar.activation(rule_row[:], FB[:, 2 * P:3 * P], ACT.Identity,
                                                 bias=half[:, 0:1]).then_inc(s_bases, 1)
                        elif step == 7:
                            act.wait_ge(s_ruled, done * RG)
                            nc.scalar.copy(hT[:], FB[0:D, 0:P]).then_inc(s_hTs, 1)

                    def rows_end(t):
                        act.wait_ge(s_xT, t + 1)
                        nc.scalar.copy(x1T[:, t * P:(t + 1) * P], FB[:, 2 * P:3 * P]).then_inc(s_xTs, 1)

                    def choice_step(t, step):
                        if step == 4:
                            act.wait_ge(s_fd, t + 1)
                            w = weight[:, t % RING, :, :]
                            nc.scalar.activation(w, w, ACT.Exp).then_inc(s_fe, 1)

                    def beside(att, t, h):
                        if att == 1 and rows_beside(t):
                            row_step(t + 1, h)
                        if queries_beside(att, t, h):
                            query_step(t + LEAD, h)
                        if att == 1 and t > LEAD and h == 1:
                            choice_step(t - 1, 4)

                    def front(t):
                        done = t + 1
                        act.wait_ge(s_q1, done)
                        for r in range(2):
                            rows = slice(r * D, (r + 1) * D)
                            last = nc.scalar.copy(q1[rows, r:H:2, :], FB[rows, :].rearrange("p (c q) -> p c q", q=P))
                        last.then_inc(s_q1s, 1)
                        attention(1, t)
                        if rows_beside(t):
                            rows_end(t + 1)

                    def query_step(t, step):
                        if step == 1:
                            act.wait_ge(s_x2T, t + 1)
                            nc.scalar.copy(x2T[:], FB[:, 0:P]).then_inc(s_x2Ts, 1)
                        elif step in (2, 3):
                            part = step - 2
                            act.wait_ge(s_sim, 2 * t + part + 1)
                            if t:
                                act.wait_ge(s_row, t * (H // EQH))
                            nc.scalar.copy(work[:, part * BANK:(part + 1) * BANK], FB[:, :]).then_inc(s_sims, 1)
                        elif step == 4:
                            act.wait_ge(s_q2, t + 1)
                            nc.scalar.mul(qT2[:, t % RING, :, :], FB[:, :].rearrange("p (c q) -> p c q", q=P),
                                          float(D) ** -0.5).then_inc(s_q2s, 1)

                    def back(t):
                        act.wait_ge(s_q2s, t + 1)
                        for r in range(2):
                            rows = slice(r * D, (r + 1) * D)
                            last = nc.scalar.copy(q2[rows, r:H:2, :], qT2[rows, t % RING, :, :])
                        last.then_inc(s_q2p, 1)
                        attention(2, t)
                        if t + LEAD == T - 1:
                            choice_step(T - 1, 4)

                    for what, t in plan:
                        if what == "embed":
                            embed(t)
                        elif what == "rows":
                            for step in range(H):
                                row_step(t, step)
                            rows_end(t)
                        elif what == "choice":
                            for step in range(H):
                                choice_step(t, step)
                        elif what == "queries":
                            for step in range(5):
                                query_step(t, step)
                        elif what == "front":
                            front(t)
                        elif what == "back":
                            back(t)

                @block.tensor
                def _(pe):
                    def attention(att, t):
                        g0, n0, n = first_chunk[att, t], first_head[att, t], n_chunks(t)
                        blocks = [min(BLK, t + 1 - BLK * c) for c in range(n)]
                        total = H * n

                        def scores(k):
                            h, c, g = k // n, k % n, g0 + k
                            if g >= 4:
                                pe.wait_ge(s_exp, g - 3)
                            if att == 2 and k % (2 * n) == 0:
                                pair = h // 2
                                pe.wait_ge(s_ks, t * PAIRS + pair + 1)
                                nc.tensor.transpose(SB[g % 4][:, 0:P], k_rows[:, pair * P:(pair + 1) * P],
                                                    ident[:]).then_inc(s_kT, 1)
                                pe.wait_ge(s_vs, t * PAIRS + pair + 1)
                                pe.wait_ge(s_kTs, t * PAIRS + pair + 1)
                            keys = slice(c * BANK, c * BANK + blocks[c] * P)
                            q = (q1 if att == 1 else q2)[:, h, :]
                            k_all = x1T[:, keys] if att == 1 else k2T[:, h // 2, keys]
                            diagonal = c == n - 1
                            last = nc.tensor.matmul(SB[g % 4][:, 0:blocks[c] * P], q, k_all, start=True, stop=not diagonal)
                            if diagonal:
                                last = nc.tensor.matmul(SB[g % 4][:, (blocks[c] - 1) * P:blocks[c] * P], ident_bf[:],
                                                        mask[:], start=False, stop=True)
                            last.then_inc(s_qk, 1)

                        def transposes(k):
                            g = g0 + k
                            pe.wait_ge(s_exp, g + 1)
                            if g >= 1:
                                pe.wait_ge(s_pt, g)
                            for j in range(blocks[k % n]):
                                last = nc.tensor.transpose(TB[:, j * P:(j + 1) * P],
                                                           probs[:, g % 4, j * P:(j + 1) * P], ident[:])
                            last.then_inc(s_tr, 1)

                        def weigh_values(k):
                            h, c, g = k // n, k % n, g0 + k
                            pe.wait_ge(s_pt, g + 1)
                            if c == 0 and n0 + h >= 2:
                                pe.wait_ge(s_acc, n0 + h - 1)
                            for j in range(blocks[c]):
                                at = c * BLK + j
                                v = x1[:, at, :] if att == 1 else v2[:, at, h, :]
                                last = nc.tensor.matmul(VB[h % 2][0:D + 1, 0:P], v, probsT[:, g % 2, j * P:(j + 1) * P],
                                                        start=at == 0, stop=at == t)
                            last.then_inc(s_pv, 1)

                        def project(h):
                            pe.wait_ge(s_zTs, n0 + h + 1)
                            nc.tensor.matmul(VB[h % 2][:, 0:D + 1], zT[:, h % 2, :], (WX1 if att == 1 else WX2)[:, h, :],
                                             start=True, stop=True).then_inc(s_y, 1)

                        for k in range(min(4, total)):
                            scores(k)
                        for k in range(total + 2):
                            values_first = n > 1 and k % n == 0
                            if values_first and k:
                                weigh_values(k - 1)
                            if k < total:
                                if k % n == 0 and att == 1 and rows_beside(t):
                                    row_step(t + 1, k // n)
                                if k % n == 0 and queries_beside(att, t, k // n):
                                    query_step(t + LEAD, k // n)
                                transposes(k)
                            if k + 4 < total:
                                scores(k + 4)
                            if 1 <= k <= total and not values_first:
                                weigh_values(k - 1)
                            if k >= 2 and (k - 1) % n == 0:
                                project((k - 1) // n - 1)

                    def row_step(t, step):
                        done = t + 1
                        if step == 0:
                            if t == 1:
                                pe.wait_ge(s_q2s, t)
                            if t % GT == 0:
                                pe.wait_ge(s_four, t // GT + 1)
                            nc.tensor.transpose(FB[0:D, 0:P], e_a[:, t // GT % 2, t % GT, :], ident[:]).then_inc(s_fT, 1)
                        elif step == 1:
                            pe.wait_ge(s_fTs, done)
                            nc.tensor.matmul(FB[:, P:2 * P], projT[:], fT[:], start=True, stop=True)
                            nc.tensor.matmul(FB[:, 2 * P:3 * P], rule_of[:, t:t + 1].to_broadcast([P, P]), ident[:],
                                             start=True, stop=True).then_inc(s_base, 1)
                        elif step < 7:
                            for g in range((step - 2) * RS, (step - 1) * RS):
                                pe.wait_ge(s_mask, t * RG + g + 1)
                                for j in range(MG):
                                    c = g * MG + j
                                    last = nc.tensor.matmul(FB[0:D, 0:P], rules[:, c, :], masked[:, g % 2, j, :],
                                                            start=c == 0, stop=c == RC - 1)
                                last.then_inc(s_ruled, 1)
                        elif step == 7:
                            pe.wait_ge(s_hTs, done)
                            nc.tensor.transpose(FB[:, P:P + D], hT[:], ident[0:D, 0:D]).then_inc(s_h0, 1)

                    def rows_end(t):
                        pe.wait_ge(s_xd, t + 1)
                        nc.tensor.transpose(FB[:, 2 * P:3 * P], xd[:].rearrange("p r f -> p (r f)"), ident[:]).then_inc(s_xT, 1)
                        pe.wait_ge(s_xTs, t + 1)

                    def front(t):
                        done = t + 1
                        if t:
                            pe.wait_ge(s_q2s, t)
                        for c in range(PAIRS):
                            last = nc.tensor.matmul(FB[:, c * P:(c + 1) * P], M1[:, c * P:(c + 1) * P],
                                                    x1T[:, t * P:(t + 1) * P], start=True, stop=True)
                        last.then_inc(s_q1, 1)
                        pe.wait_ge(s_q1s, done)
                        attention(1, t)
                        if rows_beside(t):
                            rows_end(t + 1)

                    def query_step(t, step):
                        if step == 1:
                            pe.wait_ge(s_x2, t + 1)
                            nc.tensor.transpose(FB[:, 0:P], xd[:].rearrange("p r f -> p (r f)"), ident[:]).then_inc(s_x2T, 1)
                        elif step in (2, 3):
                            part = step - 2
                            if part == 0:
                                pe.wait_ge(s_x2Ts, t + 1)
                            else:
                                pe.wait_ge(s_sims, 2 * t + 1)
                            nc.tensor.matmul(FB[:, :], x2T[:], A[:, part * BANK:(part + 1) * BANK],
                                             start=True, stop=True).then_inc(s_sim, 1)
                        elif step == 4:
                            pe.wait_ge(s_sims, 2 * t + 2)
                            for c in range(PAIRS):
                                last = nc.tensor.matmul(FB[:, c * P:(c + 1) * P], Wq[:, c * P:(c + 1) * P], x2T[:],
                                                        start=True, stop=True)
                            last.then_inc(s_q2, 1)

                    def back(t):
                        pe.wait_ge(s_q2p, t + 1)
                        attention(2, t)

                    for what, t in plan:
                        if what == "rows":
                            for step in range(H):
                                row_step(t, step)
                            rows_end(t)
                        elif what == "queries":
                            for step in range(5):
                                query_step(t, step)
                        elif what == "front":
                            front(t)
                        elif what == "back":
                            back(t)

                @block.vector
                def _(dve):
                    steps = [0]

                    def link(ins):
                        steps[0] += 1
                        ins.then_inc(s_dve, 1)
                        dve.wait_ge(s_dve, steps[0])

                    V = nc.vector

                    def divide_ids():
                        f, qa, qb, r = (work[:, n * T:(n + 1) * T] for n in range(4))
                        r0 = quotient[:]
                        inv = float(np.float32(1.0) / np.float32(VOCAB))
                        hi, lo = float(VOCAB // 256 * 256), float(VOCAB % 256)
                        dve.wait_ge(s_ids, 16)
                        link(V.tensor_copy(f, ids[:]))
                        link(V.tensor_scalar(r0, f, inv, None, ALU.mult))
                        link(V.tensor_scalar(qa.bitcast(I32), r0.bitcast(I32), -4096, None, ALU.bitwise_and))
                        link(V.tensor_tensor(qb, r0, qa, ALU.subtract))
                        link(V.scalar_tensor_tensor(r, qa, -hi, f, ALU.mult, ALU.add))
                        link(V.scalar_tensor_tensor(r, qa, -lo, r, ALU.mult, ALU.add))
                        link(V.scalar_tensor_tensor(r, qb, -hi, r, ALU.mult, ALU.add))
                        link(V.scalar_tensor_tensor(r, qb, -lo, r, ALU.mult, ALU.add))
                        link(V.scalar_tensor_tensor(r0, r, inv, r0, ALU.mult, ALU.add))
                        link(V.tensor_scalar(angular[:], freq[:], float(np.float32(2.0 * math.pi)), None, ALU.mult))

                    def embed(g):
                        shape = [P, GT, D]
                        ang, k, sn, cs = (trig[:, n, :, :] for n in range(4))
                        link(V.tensor_tensor(ang, angular[:].unsqueeze(1).to_broadcast(shape),
                                             quotient[:, g * GT:(g + 1) * GT].unsqueeze(2).to_broadcast(shape), ALU.mult))
                        link(V.tensor_scalar(k, ang, 1.0 / (2.0 * math.pi), ROUND, ALU.mult, ALU.add))
                        link(V.tensor_scalar(k, k, ROUND, None, ALU.subtract))
                        for c in two_pi_parts():
                            link(V.scalar_tensor_tensor(ang, k, -c, ang, ALU.mult, ALU.add))
                        link(V.tensor_scalar(sn, ang, 3.1415925, -3.1415925, ALU.min, ALU.max))
                        link(V.scalar_tensor_tensor(cs, sn, -1.0, sn, ALU.mult, ALU.max))
                        V.tensor_scalar(cs, cs, -1.0, math.pi / 2, ALU.mult, ALU.add).then_inc(s_angle, 1)
                        dve.wait_ge(s_trig, g + 1)
                        dve.wait_ge(s_emb[g % 2], 16 * 3 * GT * (g // 2 + 1))
                        a, bb = e_a[:, g % 2, :, :], e_b[:, g % 2, :, :]
                        V.tensor_tensor(a, a, cs, ALU.mult)
                        link(V.tensor_tensor(bb, bb, sn, ALU.mult))
                        V.tensor_copy(rule_of[:, g * GT:(g + 1) * GT], rule_i[:, g % 2, :])
                        V.tensor_tensor(a, a, bb, ALU.add).then_inc(s_four, 1)

                    def layernorm_scale(src):
                        v, y, u = rs[:, 0:1], rs[:, 1:2], rs[:, 2:3]
                        link(V.bn_stats(stats[:], src))
                        link(V.bn_aggr(meanvar[:], stats[:]))
                        link(V.tensor_scalar(v, meanvar[:, 1:2], EPS, None, ALU.add))
                        link(V.tensor_scalar(u.bitcast(I32), v.bitcast(I32), 1, None, ALU.logical_shift_right))
                        link(V.tensor_scalar(y.bitcast(I32), u.bitcast(I32), -1.0, float(RSQRT_SEED), ALU.mult, ALU.add))
                        for _ in range(3):
                            link(V.tensor_scalar(u, y, y, v, ALU.mult, ALU.mult))
                            link(V.tensor_scalar(u, u, -0.5, 1.5, ALU.mult, ALU.add))
                            link(V.tensor_tensor(y, y, u, ALU.mult))

                    def combine_at(stage, tile, place):
                        for t, h in heads_at.get((stage, tile, place), ()):
                            n = t * H + h
                            slot = n % SLOTS
                            uses = len(range(slot, T * H, SLOTS))
                            if t:
                                dve.wait_ge(s_ks, (t - 1) * PAIRS + h // 2 + 1)
                                dve.wait_ge(s_vs, (t - 1) * PAIRS + h // 2 + 1)
                            dve.wait_ge(s_g[slot], 256 * (n // SLOTS + 1))
                            w = weight[:, t % RING, h, :].unsqueeze(2).to_broadcast([P, TOPK, 2 * D])
                            rows = G[:, slot, :, :]
                            link(V.tensor_tensor(rows, rows, w, ALU.mult))
                            last = V.tensor_reduce(kv[:, h, :], rows.rearrange("p r f -> p f r"), AX, ALU.add)
                            last.then_inc(s_comb, 1)

                    def attention(att, t):
                        g0, n0, n = first_chunk[att, t], first_head[att, t], n_chunks(t)
                        widths = [min(BLK, t + 1 - BLK * c) * P for c in range(n)]
                        before, total = (h0[:], h1[:, t % RING, :]) if att == 1 else (h1[:, t % RING, :], obuf[:, t % 2, :])

                        def add(h):
                            dve.wait_ge(s_y, n0 + h + 1)
                            y = VB[h % 2]
                            link(V.reciprocal(rec[:, h % 2:h % 2 + 1], y[:, D:D + 1]))
                            last = V.scalar_tensor_tensor(total, y[:, 0:D], rec[:, h % 2:h % 2 + 1],
                                                          total if h else before, ALU.mult, ALU.add)
                            last.then_inc(s_acc, 1)
                            dve.wait_ge(s_acc, n0 + h + 1)

                        for h in range(H + 2):
                            if h < H:
                                for c in range(n):
                                    g = g0 + h * n + c
                                    dve.wait_ge(s_qk, g + 1)
                                    dst = nmax[:, h:h + 1] if n == 1 else mx[:, h % 2, c:c + 1]
                                    last = V.tensor_reduce(dst, SB[g % 4][:, 0:widths[c]], AX, ALU.max, negate=n == 1)
                                if n > 1:
                                    link(last)
                                    last = V.tensor_reduce(nmax[:, h:h + 1], mx[:, h % 2, 0:n], AX, ALU.max, negate=True)
                                last.then_inc(s_max, 1)
                            if h >= 2:
                                add(h - 2)
                            if att == 1 and rows_beside(t) and h <= H:
                                row_step(t + 1, h)
                            if queries_beside(att, t, h):
                                query_step(t + LEAD, h)
                            chosen, choice_steps = choice_beside(att, t, h)
                            for step in choice_steps:
                                choice_step(chosen, step)
                            combine_at("front" if att == 1 else "back", t, h)
                        nc.vector.sem_inc(s_h, 1)

                    def top8(values, largest, index, rank, n):
                        ranks = slice(rank, rank + 8)
                        for j in range(n):
                            last = V.max(largest[:, j, ranks], values[:, j, :])
                        link(last)
                        for j in range(n):
                            last = V.max_index(index[:, j, ranks], largest[:, j, ranks], values[:, j, :])
                        if rank + 8 < TOPK:
                            for j in range(n):
                                last = V.match_replace(values[:, j, :], largest[:, j, ranks], values[:, j, :], LOWEST)
                        link(last)

                    def row_step(t, step):
                        done = t + 1
                        if 1 <= step < 6:
                            dve.wait_ge(s_bases, done)
                            for g in range((step - 1) * RS, step * RS):
                                if t * RG + g >= 2:
                                    dve.wait_ge(s_ruled, t * RG + g - 1)
                                for j in range(MG):
                                    last = V.scalar_tensor_tensor(masked[:, g % 2, j, :], rule_row[:],
                                                                  2.0 * (g * MG + j), base2[:], ALU.is_equal, ALU.mult)
                                last.then_inc(s_mask, 1)
                        elif step == 8:
                            dve.wait_ge(s_h0, done)
                            link(V.tensor_copy(h0[:], FB[:, P:P + D]))
                            layernorm_scale(h0[:])
                            V.tensor_scalar(xd[:], h0[:].unsqueeze(1).to_broadcast([P, 2, D]), meanvar[:, 0:1],
                                            rs[:, 1:2], ALU.subtract, ALU.mult)
                            V.tensor_scalar(x1[:, t, 0:D], h0[:], meanvar[:, 0:1], rs[:, 1:2],
                                            ALU.subtract, ALU.mult).then_inc(s_xd, 1)

                    def front(t):
                        attention(1, t)

                    def query_step(t, step):
                        if step == 0:
                            h = h1[:, t % RING, :]
                            layernorm_scale(h)
                            if rows_beside(t):
                                dve.wait_ge(s_xT, t + 2)
                            V.tensor_scalar(xd[:], h.unsqueeze(1).to_broadcast([P, 2, D]), meanvar[:, 0:1], rs[:, 1:2],
                                            ALU.subtract, ALU.mult).then_inc(s_x2, 1)

                    def choice_step(t, step):
                        done = t + 1
                        w = weight[:, t % RING, :, :]
                        if step == 0:
                            dve.wait_ge(s_sims, 2 * done)
                            top8(scores_pk, sv, si, 0, NP)
                        elif step == 1:
                            top8(scores_pk, sv, si, 8, NP)
                            s0, s1, i0, i1 = sv[:, 0:H, :], sv[:, H:NP, :], si[:, 0:H, :], si[:, H:NP, :]
                            link(V.scalar_tensor_tensor(jrow[:], i1, float(NKEYS), head_row[:], ALU.mult, ALU.add))
                            for a, rows, n, at in RUNS:
                                for dst, left, right in ((cand, s0, s1), (cand_row, i0, jrow)):
                                    if rows == 1:
                                        o, l, r = (dst[:, :, at:at + n], left[:, :, a:a + 1].to_broadcast([P, H, n]),
                                                   right[:, :, 0:n])
                                    else:
                                        shape = [P, H, rows, n]
                                        o = dst[:, :, at:at + rows * n].rearrange("p h (a b) -> p h a b", b=n)
                                        l = left[:, :, a:a + rows].unsqueeze(3).to_broadcast(shape)
                                        r = right[:, :, 0:n].unsqueeze(2).to_broadcast(shape)
                                    last = V.tensor_tensor(o, l, r, ALU.add)
                            link(last)
                            link(V.tensor_tensor(cand_row[:], cand_row[:], place[:].unsqueeze(1).to_broadcast([P, H, NC]),
                                                 ALU.add))
                        elif step == 2:
                            top8(cand, fv, fpos, 0, H)
                        elif step == 3:
                            top8(cand, fv, fpos, 8, H)
                            V.tensor_tensor(w, fv[:], fv[:, :, 0:1].to_broadcast([P, H, TOPK]), ALU.subtract).then_inc(s_fd, 1)
                            link(V.tensor_scalar(fcode[:], fpos[:], float(CODE), None, ALU.mult))
                        else:
                            hs = slice((step - 4) * EQH, (step - 3) * EQH)
                            far = work[:].rearrange("p (h r c) -> p h r c", h=EQH, c=NC)
                            shape = [P, EQH, TOPK, NC]
                            link(V.tensor_tensor(far, cand_row[:, hs, :].unsqueeze(2).to_broadcast(shape),
                                                 fcode[:, hs, :].unsqueeze(3).to_broadcast(shape), ALU.subtract))
                            link(V.tensor_reduce(fcode[:, hs, :], far, AX, ALU.min, apply_absolute_value=True))
                            V.tensor_copy(row_u[:, t % RING, hs.start * TOPK:hs.stop * TOPK],
                                          fcode[:, hs, :].rearrange("p h r -> p (h r)")).then_inc(s_row, 1)
                        if step == 7:
                            dve.wait_ge(s_fe, done)
                            link(V.tensor_reduce(wsum[:], w, AX, ALU.add))
                            link(V.reciprocal(wsum[:], wsum[:]))
                            link(V.tensor_tensor(w, w, wsum[:].unsqueeze(2).to_broadcast([P, H, TOPK]), ALU.mult))

                    def back(t):
                        if t >= 2:
                            dve.wait_ge(s_out[t % 2], 16 * (t // 2))
                        attention(2, t)

                    divide_ids()
                    for what, t in plan:
                        if what == "embed":
                            embed(t)
                        elif what == "rows":
                            for step in range(H + 1):
                                row_step(t, step)
                        elif what == "choice":
                            for step in range(H):
                                choice_step(t, step)
                        elif what == "queries":
                            for step in range(5):
                                query_step(t, step)
                        elif what == "front":
                            front(t)
                        elif what == "back":
                            back(t)

        with nc.Fori(0, NB) as b:
            batch(b)
            nc.all_engine_barrier(sems_to_clear=batch_sems)


_INS = ["x", "L0_tok_a_n", "L0_tok_b_n", "L0_tok_rule_transform", "L0_tok_token_rules", "L0_tok_proj_w",
        "L0_tok_proj_b", "L0_attn_key_matrices", "L0_attn_query_matrices", "L0_attn_value_in_matrices",
        "L0_attn_value_out_matrices", "L0_ffn_Wq_pk", "L0_ffn_pk_keys", "L0_ffn_Wq", "L0_ffn_keys_table",
        "L0_ffn_values_table", "L0_ffn_Wo"]


def kernel(**inputs):
    import numpy as _np
    import concourse.bacc as _bacc
    from concourse import mybir as _mybir
    from concourse.bass_utils import run_bass_kernel_spmd as _run

    nc = _bacc.Bacc("TRN2", target_bir_lowering=False, num_devices=1)
    arrays, args = {}, []
    for name in _INS:
        a = _np.ascontiguousarray(inputs[name])
        arrays[f"in_{name}"] = a
        args.append(nc.dram_tensor(f"in_{name}", a.shape, _mybir.dt.from_np(a.dtype), kind="ExternalInput").ap())
    b, s = inputs["x"].shape
    out = nc.dram_tensor("out_rows", (b, s, inputs["L0_tok_a_n"].shape[1]), _mybir.dt.float32, kind="ExternalOutput").ap()
    lm_block(nc, *args, out)
    r = _run(nc, [arrays], core_ids=[0])
    return r.results[0]["out_rows"]
```
